# Optimizing a Trainium2 kernel written in Bass

```python
import numpy as np
import jax
import jax.numpy as jnp

def _softmax(x, axis=-1):
    return jax.nn.softmax(x, axis=axis)

def _gelu(x):
    return jax.nn.gelu(x, approximate=True)

def _silu(x):
    return jax.nn.silu(x)

def _sigmoid(x):
    return jax.nn.sigmoid(x)

def _layernorm(x, axis=-1, eps=1e-05):
    m = jnp.mean(x, axis=axis, keepdims=True)
    v = jnp.var(x, axis=axis, keepdims=True)
    return (x - m) / jnp.sqrt(v + eps)

def _scatter_add(tgt, idx, src, axis=0):
    return tgt.at[idx].add(src)

def _segment_sum(src, seg, n):
    return jax.ops.segment_sum(src, seg, n)
kernel_name = 'mk_dlrm_tower_d1_rec_r8_c3a659'

def setup_inputs(seed: int=0):
    np.random.seed(seed)
    _w = jnp.asarray

    def _rec_inputs():
        import jax
        import jax.numpy as jnp
        _tk = jax.random.key(seed)
        dense_ctx = jax.random.normal(jax.random.fold_in(_tk, 190), (2048, 16), jnp.float32)
        ids = jnp.stack([jax.random.randint(jax.random.fold_in(_tk, 200 + f), (2048,), 0, v, jnp.int32) for f, v in enumerate([1000, 1250, 12500, 12500, 125000, 125000, 1000, 1000, 1000, 125000, 125000, 1250, 1000, 12500, 1250, 1250, 12500, 1000, 1250, 125000, 1250, 1000, 125000, 1000, 125000, 1000, 1250, 1000, 1250, 1250, 1000, 12500, 125000, 1250, 125000, 1250, 1250, 1000, 1250])], axis=1)
        tbl_0 = 0.05 * jax.random.normal(jax.random.fold_in(_tk, 500 + 0), (1000, 16), jnp.float32)
        tbl_1 = 0.05 * jax.random.normal(jax.random.fold_in(_tk, 500 + 1), (1250, 16), jnp.float32)
        tbl_2 = 0.05 * jax.random.normal(jax.random.fold_in(_tk, 500 + 2), (12500, 16), jnp.float32)
        tbl_3 = 0.05 * jax.random.normal(jax.random.fold_in(_tk, 500 + 3), (12500, 16), jnp.float32)
        tbl_4 = 0.05 * jax.random.normal(jax.random.fold_in(_tk, 500 + 4), (125000, 16), jnp.float32)
        tbl_5 = 0.05 * jax.random.normal(jax.random.fold_in(_tk, 500 + 5), (125000, 16), jnp.float32)
        tbl_6 = 0.05 * jax.random.normal(jax.random.fold_in(_tk, 500 + 6), (1000, 16), jnp.float32)
        tbl_7 = 0.05 * jax.random.normal(jax.random.fold_in(_tk, 500 + 7), (1000, 16), jnp.float32)
        tbl_8 = 0.05 * jax.random.normal(jax.random.fold_in(_tk, 500 + 8), (1000, 16), jnp.float32)
        tbl_9 = 0.05 * jax.random.normal(jax.random.fold_in(_tk, 500 + 9), (125000, 16), jnp.float32)
        tbl_10 = 0.05 * jax.random.normal(jax.random.fold_in(_tk, 500 + 10), (125000, 16), jnp.float32)
        tbl_11 = 0.05 * jax.random.normal(jax.random.fold_in(_tk, 500 + 11), (1250, 16), jnp.float32)
        tbl_12 = 0.05 * jax.random.normal(jax.random.fold_in(_tk, 500 + 12), (1000, 16), jnp.float32)
        tbl_13 = 0.05 * jax.random.normal(jax.random.fold_in(_tk, 500 + 13), (12500, 16), jnp.float32)
        tbl_14 = 0.05 * jax.random.normal(jax.random.fold_in(_tk, 500 + 14), (1250, 16), jnp.float32)
        tbl_15 = 0.05 * jax.random.normal(jax.random.fold_in(_tk, 500 + 15), (1250, 16), jnp.float32)
        tbl_16 = 0.05 * jax.random.normal(jax.random.fold_in(_tk, 500 + 16), (12500, 16), jnp.float32)
        tbl_17 = 0.05 * jax.random.normal(jax.random.fold_in(_tk, 500 + 17), (1000, 16), jnp.float32)
        tbl_18 = 0.05 * jax.random.normal(jax.random.fold_in(_tk, 500 + 18), (1250, 16), jnp.float32)
        tbl_19 = 0.05 * jax.random.normal(jax.random.fold_in(_tk, 500 + 19), (125000, 16), jnp.float32)
        tbl_20 = 0.05 * jax.random.normal(jax.random.fold_in(_tk, 500 + 20), (1250, 16), jnp.float32)
        tbl_21 = 0.05 * jax.random.normal(jax.random.fold_in(_tk, 500 + 21), (1000, 16), jnp.float32)
        tbl_22 = 0.05 * jax.random.normal(jax.random.fold_in(_tk, 500 + 22), (125000, 16), jnp.float32)
        tbl_23 = 0.05 * jax.random.normal(jax.random.fold_in(_tk, 500 + 23), (1000, 16), jnp.float32)
        tbl_24 = 0.05 * jax.random.normal(jax.random.fold_in(_tk, 500 + 24), (125000, 16), jnp.float32)
        tbl_25 = 0.05 * jax.random.normal(jax.random.fold_in(_tk, 500 + 25), (1000, 16), jnp.float32)
        tbl_26 = 0.05 * jax.random.normal(jax.random.fold_in(_tk, 500 + 26), (1250, 16), jnp.float32)
        tbl_27 = 0.05 * jax.random.normal(jax.random.fold_in(_tk, 500 + 27), (1000, 16), jnp.float32)
        tbl_28 = 0.05 * jax.random.normal(jax.random.fold_in(_tk, 500 + 28), (1250, 16), jnp.float32)
        tbl_29 = 0.05 * jax.random.normal(jax.random.fold_in(_tk, 500 + 29), (1250, 16), jnp.float32)
        tbl_30 = 0.05 * jax.random.normal(jax.random.fold_in(_tk, 500 + 30), (1000, 16), jnp.float32)
        tbl_31 = 0.05 * jax.random.normal(jax.random.fold_in(_tk, 500 + 31), (12500, 16), jnp.float32)
        tbl_32 = 0.05 * jax.random.normal(jax.random.fold_in(_tk, 500 + 32), (125000, 16), jnp.float32)
        tbl_33 = 0.05 * jax.random.normal(jax.random.fold_in(_tk, 500 + 33), (1250, 16), jnp.float32)
        tbl_34 = 0.05 * jax.random.normal(jax.random.fold_in(_tk, 500 + 34), (125000, 16), jnp.float32)
        tbl_35 = 0.05 * jax.random.normal(jax.random.fold_in(_tk, 500 + 35), (1250, 16), jnp.float32)
        tbl_36 = 0.05 * jax.random.normal(jax.random.fold_in(_tk, 500 + 36), (1250, 16), jnp.float32)
        tbl_37 = 0.05 * jax.random.normal(jax.random.fold_in(_tk, 500 + 37), (1000, 16), jnp.float32)
        tbl_38 = 0.05 * jax.random.normal(jax.random.fold_in(_tk, 500 + 38), (1250, 16), jnp.float32)
        _rk = jax.random.fold_in(_tk, 7)
        W_top1 = 0.0606339 * jax.random.normal(jax.random.fold_in(_tk, 801), (272, 512), jnp.float32)
        W_top2 = 0.0441942 * jax.random.normal(jax.random.fold_in(_tk, 802), (512, 256), jnp.float32)
        W_top3 = 0.0625 * jax.random.normal(jax.random.fold_in(_tk, 803), (256, 1), jnp.float32)
        b_top1 = jnp.zeros((512,), jnp.float32)
        b_top2 = jnp.zeros((256,), jnp.float32)
        return (dense_ctx, ids, tbl_0, tbl_1, tbl_2, tbl_3, tbl_4, tbl_5, tbl_6, tbl_7, tbl_8, tbl_9, tbl_10, tbl_11, tbl_12, tbl_13, tbl_14, tbl_15, tbl_16, tbl_17, tbl_18, tbl_19, tbl_20, tbl_21, tbl_22, tbl_23, tbl_24, tbl_25, tbl_26, tbl_27, tbl_28, tbl_29, tbl_30, tbl_31, tbl_32, tbl_33, tbl_34, tbl_35, tbl_36, tbl_37, tbl_38, W_top1, b_top1, W_top2, b_top2, W_top3)
    dense_ctx, ids, tbl_0, tbl_1, tbl_2, tbl_3, tbl_4, tbl_5, tbl_6, tbl_7, tbl_8, tbl_9, tbl_10, tbl_11, tbl_12, tbl_13, tbl_14, tbl_15, tbl_16, tbl_17, tbl_18, tbl_19, tbl_20, tbl_21, tbl_22, tbl_23, tbl_24, tbl_25, tbl_26, tbl_27, tbl_28, tbl_29, tbl_30, tbl_31, tbl_32, tbl_33, tbl_34, tbl_35, tbl_36, tbl_37, tbl_38, W_top1, b_top1, W_top2, b_top2, W_top3 = _rec_inputs()

    def _L0_rec_setup():
        import jax, jax.numpy as jnp
        import numpy as np
        B, M0, D = (256, 39, 16)
        CIN_SIZE = [128, 128]

        def _cin(inputs, weights):
            X0 = inputs
            Xi = inputs
            res = []
            for W in weights:
                mi = Xi.shape[1]
                z = jnp.einsum('bmd,bnd->bdmn', X0, Xi)
                z = z.reshape(z.shape[0], z.shape[1], M0 * mi)
                Xi = jnp.einsum('bdp,po->bod', z, W)
                res.append(Xi)
            res = jnp.concatenate(res, axis=1)
            return jnp.sum(res, axis=-1)
        key = jax.random.key(seed)
        k1, k2, k3 = jax.random.split(key, 3)
        inputs = jax.random.normal(k1, (B, M0, D), dtype=jnp.float32)
        W0 = jax.random.normal(k2, (M0 * M0, CIN_SIZE[0]), dtype=jnp.float32) * 0.05
        W1 = jax.random.normal(k3, (M0 * CIN_SIZE[0], CIN_SIZE[1]), dtype=jnp.float32) * 0.05
        return {'inputs': inputs, 'W0': W0, 'W1': W1}
    _L0_rec_all = _L0_rec_setup()
    _L0_rec_in = {k: v for k, v in _L0_rec_all.items() if k in ('W0', 'W1')}
    del _L0_rec_all
    return {'dense_ctx': dense_ctx, 'ids': ids, 'tbl_0': tbl_0, 'tbl_1': tbl_1, 'tbl_2': tbl_2, 'tbl_3': tbl_3, 'tbl_4': tbl_4, 'tbl_5': tbl_5, 'tbl_6': tbl_6, 'tbl_7': tbl_7, 'tbl_8': tbl_8, 'tbl_9': tbl_9, 'tbl_10': tbl_10, 'tbl_11': tbl_11, 'tbl_12': tbl_12, 'tbl_13': tbl_13, 'tbl_14': tbl_14, 'tbl_15': tbl_15, 'tbl_16': tbl_16, 'tbl_17': tbl_17, 'tbl_18': tbl_18, 'tbl_19': tbl_19, 'tbl_20': tbl_20, 'tbl_21': tbl_21, 'tbl_22': tbl_22, 'tbl_23': tbl_23, 'tbl_24': tbl_24, 'tbl_25': tbl_25, 'tbl_26': tbl_26, 'tbl_27': tbl_27, 'tbl_28': tbl_28, 'tbl_29': tbl_29, 'tbl_30': tbl_30, 'tbl_31': tbl_31, 'tbl_32': tbl_32, 'tbl_33': tbl_33, 'tbl_34': tbl_34, 'tbl_35': tbl_35, 'tbl_36': tbl_36, 'tbl_37': tbl_37, 'tbl_38': tbl_38, 'W_top1': W_top1, 'b_top1': b_top1, 'W_top2': W_top2, 'b_top2': b_top2, 'W_top3': W_top3, 'L0_rec_W0': _L0_rec_in['W0'], 'L0_rec_W1': _L0_rec_in['W1']}

def reference(dense_ctx, ids, tbl_0, tbl_1, tbl_2, tbl_3, tbl_4, tbl_5, tbl_6, tbl_7, tbl_8, tbl_9, tbl_10, tbl_11, tbl_12, tbl_13, tbl_14, tbl_15, tbl_16, tbl_17, tbl_18, tbl_19, tbl_20, tbl_21, tbl_22, tbl_23, tbl_24, tbl_25, tbl_26, tbl_27, tbl_28, tbl_29, tbl_30, tbl_31, tbl_32, tbl_33, tbl_34, tbl_35, tbl_36, tbl_37, tbl_38, W_top1, b_top1, W_top2, b_top2, W_top3, L0_rec_W0, L0_rec_W1):
    import jax
    import jax.numpy as jnp

    def _L0_rec_ref(inputs, W0, W1):
        import jax, jax.numpy as jnp
        import numpy as np
        B, M0, D = (256, 39, 16)
        CIN_SIZE = [128, 128]

        def _cin(inputs, weights):
            X0 = inputs
            Xi = inputs
            res = []
            for W in weights:
                mi = Xi.shape[1]
                z = jnp.einsum('bmd,bnd->bdmn', X0, Xi)
                z = z.reshape(z.shape[0], z.shape[1], M0 * mi)
                Xi = jnp.einsum('bdp,po->bod', z, W)
                res.append(Xi)
            res = jnp.concatenate(res, axis=1)
            return jnp.sum(res, axis=-1)
        return _cin(inputs, [W0, W1])
    e = jnp.stack([tbl_0[ids[:, 0]], tbl_1[ids[:, 1]], tbl_2[ids[:, 2]], tbl_3[ids[:, 3]], tbl_4[ids[:, 4]], tbl_5[ids[:, 5]], tbl_6[ids[:, 6]], tbl_7[ids[:, 7]], tbl_8[ids[:, 8]], tbl_9[ids[:, 9]], tbl_10[ids[:, 10]], tbl_11[ids[:, 11]], tbl_12[ids[:, 12]], tbl_13[ids[:, 13]], tbl_14[ids[:, 14]], tbl_15[ids[:, 15]], tbl_16[ids[:, 16]], tbl_17[ids[:, 17]], tbl_18[ids[:, 18]], tbl_19[ids[:, 19]], tbl_20[ids[:, 20]], tbl_21[ids[:, 21]], tbl_22[ids[:, 22]], tbl_23[ids[:, 23]], tbl_24[ids[:, 24]], tbl_25[ids[:, 25]], tbl_26[ids[:, 26]], tbl_27[ids[:, 27]], tbl_28[ids[:, 28]], tbl_29[ids[:, 29]], tbl_30[ids[:, 30]], tbl_31[ids[:, 31]], tbl_32[ids[:, 32]], tbl_33[ids[:, 33]], tbl_34[ids[:, 34]], tbl_35[ids[:, 35]], tbl_36[ids[:, 36]], tbl_37[ids[:, 37]], tbl_38[ids[:, 38]]], axis=1)
    z = _L0_rec_ref(e, L0_rec_W0, L0_rec_W1)
    z = z.reshape(z.shape[0], -1)
    h = jnp.concatenate([z, dense_ctx], axis=1)
    h = jnp.maximum(h @ W_top1 + b_top1, 0.0)
    h = jnp.maximum(h @ W_top2 + b_top2, 0.0)
    y = h @ W_top3
    return y

_drawn_inputs = setup_inputs


def setup_inputs(seed=0):
    import zlib

    import numpy as np

    out = dict(_drawn_inputs(seed))
    spreads = {'b_top1': (0.0, 0.1), 'b_top2': (0.0, 0.1)}
    factors = {'tbl_0': 4.73,
     'tbl_1': 5.096,
     'tbl_2': 4.778,
     'tbl_3': 4.89,
     'tbl_4': 5.072,
     'tbl_5': 5.033,
     'tbl_6': 4.721,
     'tbl_7': 4.87,
     'tbl_8': 4.947,
     'tbl_9': 4.482,
     'tbl_10': 5.142,
     'tbl_11': 4.948,
     'tbl_12': 4.611,
     'tbl_13': 4.404,
     'tbl_14': 4.701,
     'tbl_15': 4.867,
     'tbl_16': 5.071,
     'tbl_17': 4.909,
     'tbl_18': 5.043,
     'tbl_19': 5.257,
     'tbl_20': 4.966,
     'tbl_21': 4.949,
     'tbl_22': 4.85,
     'tbl_23': 4.776,
     'tbl_24': 4.554,
     'tbl_25': 4.54,
     'tbl_26': 5.05,
     'tbl_27': 5.105,
     'tbl_28': 4.838,
     'tbl_29': 4.625,
     'tbl_30': 5.026,
     'tbl_31': 4.465,
     'tbl_32': 4.956,
     'tbl_33': 4.819,
     'tbl_34': 4.756,
     'tbl_35': 4.885,
     'tbl_36': 4.896,
     'tbl_37': 4.903,
     'tbl_38': 5.258,
     'L0_rec_W1': 5.119}
    for name, (base, spread) in spreads.items():
        noise = np.random.default_rng([zlib.crc32(name.encode()), seed]).standard_normal(out[name].shape)
        drawn = base * np.exp(spread * noise) if base else spread * noise
        out[name] = jnp.asarray(drawn.astype(out[name].dtype))
    for name, factor in factors.items():
        out[name] = (out[name] * factor).astype(out[name].dtype)
    return out
```

```python
import numpy as np
import concourse.bass as bass
from concourse import mybir
from contextlib import ExitStack

F32, BF16, I32 = mybir.dt.float32, mybir.dt.bfloat16, mybir.dt.int32
ACT, ALU = mybir.ActivationFunctionType, mybir.AluOpType

BATCH, FIELDS, DIM = 2048, 39, 16
OUT = 128
DENSE, HID1, HID2 = 16, 512, 256
P = 128
TILE = 128
SUPER = 256
CHUNK = 32
COLS = CHUNK * DIM
N_SUPER = BATCH // SUPER
CHUNKS = SUPER // CHUNK
TILE_CHUNKS = TILE // CHUNK
PARTS = 3
ROWS = PARTS * FIELDS
SHIFTS = FIELDS // 2 + 1
GROUPS = -(-SHIFTS // PARTS)
LAST_ROWS = (SHIFTS - PARTS * (GROUPS - 1)) * FIELDS
SUBS = COLS // P
SUB_SAMPLES = P // DIM
MOMENTS = FIELDS + 1
TURN = DIM // 2
Z_BUFS = 4
SPLIT_AT, TURN_AT = 2, (2, 3)
GATHERED = FIELDS * 16
CONST_COLS = (GROUPS + 1) * ROWS


def group_rows(g):
    return ROWS if g < GROUPS - 1 else LAST_ROWS


def tower(nc, dense_t, ids, tables, pair_w, w1, w_top1a, w_top1b, b_top1, w_top2, b_top2, w_top3,
          select_const, ident_const, mask_const, out):
    ctx = ExitStack()
    with ctx:
        def sb(name, shape, dt=F32):
            return ctx.enter_context(nc.sbuf_tensor(name, shape, dt))

        def sem(name):
            return ctx.enter_context(nc.semaphore(name))

        pair_raw = sb("pair_raw", [ROWS, GROUPS, 2, OUT])
        w0_sb = sb("w0_sb", [ROWS, GROUPS, OUT])
        w1_sb = sb("w1_sb", [OUT, FIELDS, OUT])
        top1a_sb = sb("top1a_sb", [P, 2, HID1])
        top1b_sb = sb("top1b_sb", [DENSE, HID1])
        top2_sb = sb("top2_sb", [P, HID1 // P, HID2])
        top3_sb = sb("top3_sb", [P, HID2 // P])
        bias1_sb = sb("bias1_sb", [P, HID1 // P])
        bias2_sb = sb("bias2_sb", [P, HID2 // P])
        dense_sb = sb("dense_sb", [DENSE, BATCH])
        select_raw = sb("select_raw", [ROWS, CONST_COLS])
        select_sb = sb("select_sb", [ROWS, CONST_COLS], BF16)
        ident_raw = sb("ident_raw", [P, P])
        ident_sb = sb("ident_sb", [P, P], BF16)
        mask_sb = sb("mask_sb", [P, SUB_SAMPLES])

        idx_sb = sb("idx_sb", [P, 2, FIELDS], I32)
        emb = sb("emb", [P, 2, FIELDS * DIM])
        rest = sb("rest", [P, FIELDS * DIM])
        parts = sb("parts", [P, PARTS, FIELDS * DIM], BF16)
        cols = sb("cols", [ROWS, 2, TILE * DIM], BF16)
        base = sb("base", [ROWS, 2, COLS])
        pairs = sb("pairs", [ROWS, Z_BUFS, COLS])
        x1_sb = sb("x1_sb", [P, 2, SUBS * OUT])
        diag = sb("diag", [P, 2, SUBS, SUB_SAMPLES, MOMENTS])
        moments = sb("moments", [OUT, MOMENTS, SUPER])
        res_sb = sb("res_sb", [P, 2, SUPER])
        hid1_sb = sb("hid1_sb", [P, HID1 // P, SUPER])
        hid2_sb = sb("hid2_sb", [P, HID2 // P, SUPER])
        y_sb = sb("y_sb", [1, SUPER])

        shift_ps = [ctx.enter_context(nc.psum_tensor(f"shift_ps{i}", [P, COLS], F32)) for i in range(2)]
        x1_ps = [ctx.enter_context(nc.psum_tensor(f"x1_ps{i}", [P, SUBS * OUT], F32)) for i in range(2)]
        mom_ps = [ctx.enter_context(nc.psum_tensor(f"mom_ps{i}", [P, 512], F32)) for i in range(2)]
        misc_ps = ctx.enter_context(nc.psum_tensor("misc_ps", [P, 512], F32))
        top_ps = ctx.enter_context(nc.psum_tensor("top_ps", [P, 2, SUPER], F32))
        turn_ps = misc_ps[:, :].bitcast(BF16).rearrange("p (d b) -> p d b", b=TILE)
        MOM = SUB_SAMPLES * MOMENTS

        idx_loaded = [sem(f"idx_loaded{t}") for t in range(2)]
        gathered = [sem(f"gathered{t}") for t in range(2)]
        sel_loaded, pair_loaded, w1_loaded, top_loaded = (
            sem("sel_loaded"), sem("pair_loaded"), sem("w1_loaded"), sem("top_loaded"))
        const_ready, ones_ready, w0_ready = sem("const_ready"), sem("ones_ready"), sem("w0_ready")
        high_done, rest_done, middle_done, split_done = (
            sem("high_done"), sem("rest_done"), sem("middle_done"), sem("split_done"))
        turned, cols_done = sem("turned"), sem("cols_done")
        base_sel, base_done = sem("base_sel"), sem("base_done")
        shift_sel, pairs_done, pairs_used = sem("shift_sel"), sem("pairs_done"), sem("pairs_used")
        x1_done = sem("x1_done")
        diag_sel, diag_done = sem("diag_sel"), sem("diag_done")
        mom_sum, mom_done = sem("mom_sum"), sem("mom_done")
        cin2_sum, res_done = sem("cin2_sum"), sem("res_done")
        hid1_sum, hid1_done = sem("hid1_sum"), sem("hid1_done")
        hid2_sum, hid2_done = sem("hid2_sum"), sem("hid2_done")
        y_sum, y_done, y_stored = sem("y_sum"), sem("y_done"), sem("y_stored")

        def at_least(eng, semaphore, value):
            if not isinstance(value, int) or value > 0:
                eng.wait_ge(semaphore, value)

        def over_superblocks(eng, one):
            one(0)
            with eng.Fori(1, N_SUPER - 1) as sb_i:
                one(sb_i)
            one(N_SUPER - 1)

        def is_last(s):
            return isinstance(s, int) and s == N_SUPER - 1

        block = ctx.enter_context(nc.Block())

        @block.sync
        def _(sp):
            def load_indices(s, t):
                sp.dma_start(idx_sb[:, t, :], ids[bass.ds((2 * s + t) * TILE, TILE), :]).then_inc(
                    idx_loaded[t], 16)

            load_indices(0, 0)
            sp.dma_start(select_raw[:, :], select_const).then_inc(sel_loaded, 16)
            sp.dma_start(ident_raw[:, :], ident_const).then_inc(sel_loaded, 16)
            sp.dma_start(mask_sb[:, :], mask_const).then_inc(sel_loaded, 16)
            load_indices(0, 1)
            sp.dma_start(pair_raw[:, :, :, :], pair_w).then_inc(pair_loaded, 16)
            sp.dma_start(w1_sb[:, :, :], w1).then_inc(w1_loaded, 16)
            for dst, src in ((top1a_sb, w_top1a), (top1b_sb, w_top1b), (top2_sb, w_top2),
                             (top3_sb, w_top3), (bias1_sb, b_top1), (bias2_sb, b_top2),
                             (dense_sb, dense_t)):
                sp.dma_start(dst.ap(), src).then_inc(top_loaded, 16)

            def store_y(s):
                at_least(sp, y_done, s + 1)
                sp.dma_start(out[bass.ds(s * SUPER, SUPER), :].rearrange("b o -> o b"),
                             y_sb[:, :]).then_inc(y_stored, 16)

            def superblock(s):
                if not is_last(s):
                    for t in range(2):
                        at_least(sp, gathered[t], GATHERED * (s + 1))
                        load_indices(s + 1, t)
                if not (isinstance(s, int) and s == 0):
                    store_y(s - 1)

            over_superblocks(sp, superblock)
            store_y(N_SUPER - 1)
            sp.wait_ge(y_stored, 16 * N_SUPER)

        @block.gpsimd
        def _(pool):
            nc.gpsimd.memset(diag[:, 0], 0.0).then_inc(ones_ready, 1)
            nc.gpsimd.memset(diag[:, 1], 0.0).then_inc(ones_ready, 1)

            def superblock(s):
                for t in range(2):
                    for f in range(FIELDS):
                        pool.indirect_dma_start(
                            out=emb[:, t, f * DIM:(f + 1) * DIM], out_offset=None, in_=tables[f],
                            in_offset=bass.IndirectOffsetOnAxis(ap=idx_sb[:, t, f:f + 1], axis=0),
                        ).then_inc(gathered[t], 16)
                if not is_last(s):
                    pool.wait_ge(idx_loaded[0], 16 * (s + 2))
                    pool.wait_ge(idx_loaded[1], 16 * (s + 2))
                    pool.wait_ge(rest_done, 2 * (s + 1))

            pool.wait_ge(idx_loaded[0], 16)
            pool.wait_ge(idx_loaded[1], 16)
            over_superblocks(pool, superblock)

        @block.scalar
        def _(act):
            act.wait_ge(sel_loaded, 48)
            nc.scalar.copy(select_sb[:, :], select_raw[:, :]).then_inc(const_ready, 1)
            nc.scalar.copy(ident_sb[:, :], ident_raw[:, :]).then_inc(const_ready, 1)

            def high_part(s, t):
                act.wait_ge(gathered[t], GATHERED * (s + 1))
                at_least(act, turned, 2 * (2 * s + t))
                nc.scalar.copy(parts[:, 0, :], emb[:, t, :]).then_inc(high_done, 1)

            def middle_part(s, t):
                act.wait_ge(rest_done, 2 * s + t + 1)
                nc.scalar.copy(parts[:, 1, :], rest[:, :]).then_inc(middle_done, 1)

            def store_cols(s, t, half):
                act.wait_ge(turned, 2 * (2 * s + t) + half + 1)
                dst = cols[:, t, :].rearrange("p (b d) -> p b d", d=DIM)[:, :, half * TURN:(half + 1) * TURN]
                nc.scalar.copy(dst, turn_ps[:ROWS].rearrange("p d b -> p b d")).then_inc(cols_done, 1)

            def store_base(c, k):
                act.wait_ge(base_sel, c + 1)
                at_least(act, pairs_done, GROUPS * (c - 1))
                nc.scalar.copy(base[:, k % 2, :], misc_ps[:ROWS, :]).then_inc(base_done, 1)

            def store_x1(c, k):
                act.wait_ge(pairs_used, GROUPS * (c + 1))
                at_least(act, mom_sum, SUBS * (c - 1))
                nc.scalar.copy(x1_sb[:, k % 2, :], x1_ps[k % 2][:, :]).then_inc(x1_done, 1)

            def store_moments(c, k, j):
                act.wait_ge(mom_sum, SUBS * c + j + 1)
                first = (k * SUBS + j) * SUB_SAMPLES
                nc.scalar.copy(moments[:, :, first:first + SUB_SAMPLES],
                               mom_ps[j % 2][:, :MOM].rearrange("p (b m) -> p m b", m=MOMENTS)).then_inc(mom_done, 1)

            def store_results(s):
                act.wait_ge(cin2_sum, s + 1)
                act.wait_ge(mom_done, SUBS * CHUNKS * (s + 1))
                nc.scalar.copy(res_sb[:, 0, :], moments[:, FIELDS, :]).then_inc(res_done, 1)
                nc.scalar.copy(res_sb[:, 1, :], top_ps[:, 0, :]).then_inc(res_done, 1)

            def hidden1(s, half):
                act.wait_ge(hid1_sum, 2 * s + half + 1)
                for j in range(2):
                    o = 2 * half + j
                    nc.scalar.activation(hid1_sb[:, o, :], top_ps[:, j, :], ACT.Relu,
                                         bias=bias1_sb[:, o:o + 1]).then_inc(hid1_done, 1)

            def hidden2(s):
                act.wait_ge(hid2_sum, s + 1)
                for j in range(HID2 // P):
                    nc.scalar.activation(hid2_sb[:, j, :], top_ps[:, j, :], ACT.Relu,
                                         bias=bias2_sb[:, j:j + 1]).then_inc(hid2_done, 1)

            def store_result(s):
                act.wait_ge(y_sum, s + 1)
                at_least(act, y_stored, 16 * s)
                nc.scalar.copy(y_sb[:, :], top_ps[0:1, 0, :]).then_inc(y_done, 1)

            TOP_STEPS = [store_results, lambda s: hidden1(s, 0), lambda s: hidden1(s, 1), hidden2, store_result]

            def superblock(s):
                first = isinstance(s, int) and s == 0
                for k in range(CHUNKS):
                    c = CHUNKS * s + k
                    before = not (first and k == 0)
                    after = not (is_last(s) and k == CHUNKS - 1)
                    split = k % TILE_CHUNKS == SPLIT_AT and not (is_last(s) and k // TILE_CHUNKS)
                    turn = k % TILE_CHUNKS in TURN_AT and not (is_last(s) and k // TILE_CHUNKS)
                    t = (k // TILE_CHUNKS + 1) % 2
                    s_t = s if t else s + 1
                    k1 = (k - 1) % CHUNKS
                    if before:
                        store_x1(c - 1, k1)
                        store_moments(c - 1, k1, 0)
                    if turn and k % TILE_CHUNKS == TURN_AT[1]:
                        store_cols(s_t, t, 1)
                    if after:
                        store_base(c + 1, k + 1)
                    if split:
                        high_part(s_t, t)
                    if before:
                        store_moments(c - 1, k1, 1)
                    if split:
                        middle_part(s_t, t)
                    if before:
                        store_moments(c - 1, k1, 2)
                        store_moments(c - 1, k1, 3)
                    if turn and k % TILE_CHUNKS == TURN_AT[0]:
                        store_cols(s_t, t, 0)
                    if not first and k < len(TOP_STEPS):
                        TOP_STEPS[k](s - 1)

            high_part(0, 0)
            middle_part(0, 0)
            store_cols(0, 0, 0)
            store_cols(0, 0, 1)
            store_base(0, 0)
            act.wait_ge(top_loaded, 7 * 16)
            over_superblocks(act, superblock)
            c = N_SUPER * CHUNKS - 1
            store_x1(c, CHUNKS - 1)
            for j in range(SUBS):
                store_moments(c, CHUNKS - 1, j)
            for step in TOP_STEPS:
                step(N_SUPER - 1)

        @block.vector
        def _(dve):
            def rest_part(s, t):
                dve.wait_ge(high_done, 2 * s + t + 1)
                nc.vector.tensor_tensor(rest[:, :], emb[:, t, :], parts[:, 0, :], ALU.subtract).then_inc(rest_done, 1)

            def low_part(s, t):
                dve.wait_ge(middle_done, 2 * s + t + 1)
                nc.vector.tensor_tensor(parts[:, 2, :], rest[:, :], parts[:, 1, :], ALU.subtract).then_inc(split_done, 1)

            def multiply(c, k, g):
                n, nk = GROUPS * c + g, GROUPS * k + g
                if g == 0:
                    dve.wait_ge(base_done, c + 1)
                dve.wait_ge(shift_sel, n + 1)
                at_least(dve, pairs_used, n + 1 - Z_BUFS)
                r = group_rows(g)
                nc.vector.tensor_tensor(pairs[:r, nk % Z_BUFS, :], base[:r, k % 2, :], shift_ps[nk % 2][:r, :],
                                        ALU.mult).then_inc(pairs_done, 1)

            def fill_diagonal(c, k):
                dve.wait_ge(diag_sel, c + 1)
                at_least(dve, mom_sum, SUBS * (c - 1))
                fields = misc_ps[:, :SUBS * FIELDS].rearrange("p (j m) -> p j m", m=FIELDS)
                shape = [P, SUBS, SUB_SAMPLES, FIELDS]
                nc.vector.tensor_tensor(
                    diag[:, k % 2, :, :, 0:FIELDS], fields.unsqueeze(2).to_broadcast(shape),
                    mask_sb[:, :].unsqueeze(1).unsqueeze(3).to_broadcast(shape), ALU.mult,
                ).then_inc(diag_done, 1)

            dve.wait_ge(ones_ready, 2)
            dve.wait_ge(sel_loaded, 48)
            for b in range(2):
                nc.vector.tensor_copy(diag[:, b, :, :, FIELDS],
                                      mask_sb[:, :].unsqueeze(1).to_broadcast([P, SUBS, SUB_SAMPLES])).then_inc(ones_ready, 1)
            dve.wait_ge(pair_loaded, 16)
            nc.vector.tensor_tensor(w0_sb[:, :, :], pair_raw[:, :, 0, :], pair_raw[:, :, 1, :], ALU.add).then_inc(w0_ready, 1)
            rest_part(0, 0)
            low_part(0, 0)

            def superblock(s):
                for k in range(CHUNKS):
                    c = CHUNKS * s + k
                    split = k % TILE_CHUNKS == SPLIT_AT and not (is_last(s) and k // TILE_CHUNKS)
                    t = (k // TILE_CHUNKS + 1) % 2
                    s_t = s if t else s + 1
                    for g in range(GROUPS):
                        multiply(c, k, g)
                        if split and g == 3:
                            rest_part(s_t, t)
                        if split and g == 5:
                            low_part(s_t, t)
                    fill_diagonal(c, k)

            over_superblocks(dve, superblock)

        @block.tensor
        def _(pe):
            mm = nc.tensor.matmul

            def turn(s, t, half):
                pe.wait_ge(split_done, 2 * s + t + 1)
                by_dim = parts[:, :, :].rearrange("p a (m d) -> p d (a m)", d=DIM)
                for i in range(TURN):
                    last = nc.tensor.transpose(turn_ps[:ROWS, i, :], by_dim[:, half * TURN + i, :], ident_sb[:, :])
                last.then_inc(turned, 1)

            def column_range(k):
                first = k % TILE_CHUNKS * COLS
                return cols[:, k // TILE_CHUNKS % 2, first:first + COLS]

            def select_base(c, k):
                mm(misc_ps[:ROWS, :], select_sb[:, GROUPS * ROWS:], column_range(k),
                   start=True, stop=True).then_inc(base_sel, 1)

            def select_shift(k, g):
                r = group_rows(g)
                mm(shift_ps[(GROUPS * k + g) % 2][:r, :], select_sb[:, g * ROWS:g * ROWS + r], column_range(k),
                   start=True, stop=True).then_inc(shift_sel, 1)

            def select_diagonal(k):
                for j in range(SUBS):
                    last = mm(misc_ps[:, j * FIELDS:(j + 1) * FIELDS], column_range(k)[:, j * P:(j + 1) * P],
                              select_sb[:, GROUPS * ROWS:GROUPS * ROWS + FIELDS], start=True, stop=True)
                last.then_inc(diag_sel, 1)

            def cin1(c, k, g):
                r = group_rows(g)
                if g == 0:
                    at_least(pe, x1_done, c - 1)
                for j in range(SUBS):
                    last = mm(x1_ps[k % 2][:, j * OUT:(j + 1) * OUT],
                              pairs[:r, (GROUPS * k + g) % Z_BUFS, j * P:(j + 1) * P], w0_sb[:r, g, :],
                              start=(g == 0 and j == 0), stop=(g == GROUPS - 1), skip_group_check=True)
                last.then_inc(pairs_used, 1)

            def sum_moments(c, k, j):
                if j == 0:
                    pe.wait_ge(x1_done, c + 1)
                    pe.wait_ge(diag_done, c + 1)
                at_least(pe, mom_done, SUBS * c + j - 1)
                mm(mom_ps[j % 2][:, :MOM], x1_sb[:, k % 2, j * OUT:(j + 1) * OUT], diag[:, k % 2, j, :, :],
                   start=True, stop=True).then_inc(mom_sum, 1)

            def cin2(s):
                pe.wait_ge(mom_done, SUBS * CHUNKS * (s + 1))
                at_least(pe, y_done, s)
                for m in range(FIELDS):
                    last = mm(top_ps[:, 0, :], w1_sb[:, m, :], moments[:, m, :], start=(m == 0), stop=(m == FIELDS - 1))
                last.then_inc(cin2_sum, 1)

            def hidden1(s, half):
                if half:
                    pe.wait_ge(hid1_done, 4 * s + 2)
                else:
                    pe.wait_ge(res_done, 2 * (s + 1))
                for j in range(2):
                    o = (2 * half + j) * P
                    for i in range(2):
                        mm(top_ps[:, j, :], top1a_sb[:, i, o:o + P], res_sb[:, i, :], start=(i == 0), stop=False)
                    last = mm(top_ps[:, j, :], top1b_sb[:, o:o + P], dense_sb[:, bass.ds(s * SUPER, SUPER)],
                              start=False, stop=True)
                last.then_inc(hid1_sum, 1)

            def hidden2(s):
                pe.wait_ge(hid1_done, 4 * (s + 1))
                for j in range(HID2 // P):
                    for i in range(HID1 // P):
                        last = mm(top_ps[:, j, :], top2_sb[:, i, j * P:(j + 1) * P], hid1_sb[:, i, :],
                                  start=(i == 0), stop=(i == HID1 // P - 1))
                last.then_inc(hid2_sum, 1)

            def result(s):
                pe.wait_ge(hid2_done, 2 * (s + 1))
                for i in range(HID2 // P):
                    last = mm(top_ps[0:1, 0, :], top3_sb[:, i:i + 1], hid2_sb[:, i, :],
                              start=(i == 0), stop=(i == HID2 // P - 1))
                last.then_inc(y_sum, 1)

            TOP_STEPS = [cin2, lambda s: hidden1(s, 0), lambda s: hidden1(s, 1), hidden2, result]

            pe.wait_ge(const_ready, 2)
            turn(0, 0, 0)
            pe.wait_ge(cols_done, 1)
            turn(0, 0, 1)
            pe.wait_ge(cols_done, 2)
            select_base(0, 0)
            select_shift(0, 0)
            select_shift(0, 1)
            pe.wait_ge(w0_ready, 1)
            pe.wait_ge(ones_ready, 4)
            pe.wait_ge(w1_loaded, 16)
            pe.wait_ge(top_loaded, 7 * 16)

            def superblock(s):
                first = isinstance(s, int) and s == 0
                for k in range(CHUNKS):
                    c = CHUNKS * s + k
                    before = not (first and k == 0)
                    after = not (is_last(s) and k == CHUNKS - 1)
                    turning = k % TILE_CHUNKS in TURN_AT and not (is_last(s) and k // TILE_CHUNKS)
                    t = (k // TILE_CHUNKS + 1) % 2
                    s_t = s if t else s + 1
                    for g in range(GROUPS):
                        pe.wait_ge(pairs_done, GROUPS * c + g + 1)
                        ahead = GROUPS * k + g + 2
                        if after or g + 2 < GROUPS:
                            select_shift(ahead // GROUPS, ahead % GROUPS)
                        cin1(c, k, g)
                        if g == 1 and turning and k % TILE_CHUNKS == TURN_AT[1]:
                            pe.wait_ge(diag_done, c)
                            pe.wait_ge(cols_done, 2 * (2 * s_t + t) + 1)
                            turn(s_t, t, 1)
                        if g == 2 and after:
                            at_least(pe, diag_done, c)
                            pe.wait_ge(cols_done, 2 * (2 * s + (k + 1) // TILE_CHUNKS + 1))
                            select_base(c + 1, k + 1)
                        if 1 <= g <= SUBS and before:
                            sum_moments(c - 1, (k - 1) % CHUNKS, g - 1)
                        if g == 4:
                            pe.wait_ge(base_done, c + (2 if after else 1))
                            select_diagonal(k)
                        if g == GROUPS - 1 and turning and k % TILE_CHUNKS == TURN_AT[0]:
                            pe.wait_ge(diag_done, c + 1)
                            turn(s_t, t, 0)
                    if not first and k < len(TOP_STEPS):
                        TOP_STEPS[k](s - 1)

            over_superblocks(pe, superblock)
            c = N_SUPER * CHUNKS - 1
            for j in range(SUBS):
                sum_moments(c, CHUNKS - 1, j)
            for step in TOP_STEPS:
                step(N_SUPER - 1)


def select_constant():
    part_field = np.arange(ROWS) % FIELDS
    blocks = []
    for g in range(GROUPS + 1):
        shift, m = np.divmod(np.arange(ROWS), FIELDS)
        wanted = (m + PARTS * g + shift) % FIELDS if g < GROUPS else m
        blocks.append(part_field[:, None] == wanted[None, :])
    return np.concatenate(blocks, axis=1).astype(np.float32)


def pair_rows():
    shift, m = np.divmod(np.arange(ROWS), FIELDS)
    s = shift[:, None] + PARTS * np.arange(GROUPS)[None, :]
    n = (m[:, None] + s) % FIELDS
    return m[:, None] * FIELDS + n, n * FIELDS + m[:, None], s


def kernel(**inputs):
    import concourse.bacc as bacc
    from concourse.bass_utils import run_bass_kernel_spmd

    a = {k: np.ascontiguousarray(v) for k, v in inputs.items()}
    w0, rows = a["L0_rec_W0"], pair_rows()
    pair_w = np.stack([w0[rows[0]], w0[rows[1]]], axis=2)
    pair_w[rows[2] == 0, 1] = 0
    pair_w[rows[2] >= SHIFTS] = 0
    arrays = {
        "dense_t": a["dense_ctx"].T,
        "ids": a["ids"],
        **{f"tbl_{f}": a[f"tbl_{f}"] for f in range(FIELDS)},
        "pair_w": pair_w,
        "w1": a["L0_rec_W1"].reshape(FIELDS, OUT, OUT).transpose(1, 0, 2),
        "w_top1a": a["W_top1"][:2 * P].reshape(2, P, HID1).transpose(1, 0, 2),
        "w_top1b": a["W_top1"][2 * P:],
        "b_top1": a["b_top1"].reshape(HID1 // P, P).T,
        "w_top2": a["W_top2"].reshape(HID1 // P, P, HID2).transpose(1, 0, 2),
        "b_top2": a["b_top2"].reshape(HID2 // P, P).T,
        "w_top3": a["W_top3"][:, 0].reshape(HID2 // P, P).T,
        "select_const": select_constant(),
        "ident_const": np.eye(P, dtype=np.float32),
        "mask_const": (np.arange(P)[:, None] // DIM == np.arange(SUB_SAMPLES)).astype(np.float32),
    }
    arrays = {f"in_{k}": np.ascontiguousarray(v) for k, v in arrays.items()}
    nc = bacc.Bacc("TRN2", target_bir_lowering=False, num_devices=1)
    ap = {k[3:]: nc.dram_tensor(k, v.shape, mybir.dt.from_np(v.dtype), kind="ExternalInput").ap()
          for k, v in arrays.items()}
    out = nc.dram_tensor("out_y", (BATCH, 1), F32, kind="ExternalOutput").ap()
    tower(nc, ap["dense_t"], ap["ids"], [ap[f"tbl_{f}"] for f in range(FIELDS)], ap["pair_w"], ap["w1"],
          ap["w_top1a"], ap["w_top1b"], ap["b_top1"], ap["w_top2"], ap["b_top2"], ap["w_top3"],
          ap["select_const"], ap["ident_const"], ap["mask_const"], out)
    r = run_bass_kernel_spmd(nc, [arrays], core_ids=[0])
    return r.results[0]["out_y"]
```

```python
import numpy as np
import concourse.bass as bass
from concourse import mybir
from contextlib import ExitStack

F32, F32R, BF16, I32 = mybir.dt.float32, mybir.dt.float32r, mybir.dt.bfloat16, mybir.dt.int32
ACT, ALU = mybir.ActivationFunctionType, mybir.AluOpType

BATCH, FIELDS, DIM = 2048, 39, 16
OUT = 128
DENSE, HID1, HID2 = 16, 512, 256
P = 128
TILE = 128
SUPER = 256
CHUNK = 32
COLS = CHUNK * DIM
N_SUPER = BATCH // SUPER
CHUNKS = SUPER // CHUNK
TILE_CHUNKS = TILE // CHUNK
PARTS = 3
ROWS = PARTS * FIELDS
ROTATIONS = ((0, 1, 6, 31, 0), (0, 2, 12, 23, 13), (0, 3, 7, 22))
SLOTS = 5
SLOT_DMAS = [16 * sum(u < len(r) for r in ROTATIONS) for u in range(SLOTS)]
SLOT_PAIRS = ((0, 1), (0, 2), (1, 2), (0, 3), (1, 3), (2, 3), (0, 4))
GROUPS = len(SLOT_PAIRS)
LAST_ROWS = 2 * FIELDS
SUBS = COLS // P
SUB_SAMPLES = P // DIM
MOMENTS = FIELDS + 1
TURN = DIM // 2
PAIR_BUFS = 4
Z_BUFS = 7
HIGH_AHEAD = 4
LOW_LAG = 2
MOMENTS_AT = 3
TURN_X1_AT = 1
DIAG_AT, DIAG_EARLY = 6, 4
TOP_AT = {(4, 1): 0, (4, 4): 1, (CHUNKS, 1): 2, (CHUNKS, 5): 3}
TOP_AT_LAST = {(4, 1): 0, (4, 4): 1, (6, 1): 2, (6, 5): 3}
CIN2_AT = 1
CIN2_STEP = -(-FIELDS // (GROUPS * (TILE_CHUNKS - 1) - CIN2_AT))
GATHERED = FIELDS * 16

def in_first_tile(k, start):
    return start and k < TILE_CHUNKS


def split_at(k, start, what):
    if in_first_tile(k, start):
        steps = {"high": (2, 0), "rest": (2, 5), "middle": (2, 3), "low": (3, 1)}
    else:
        steps = {"high": (1, 3), "rest": (2, 1), "middle": (1, 5), "low": (2, 3)}
    chunk, group = steps[what]
    return group if k % TILE_CHUNKS == chunk else None


def shared_uses(k, start, last):
    at = k % TILE_CHUNKS
    if in_first_tile(k, start):
        uses = {2: [(1, "diag")], 3: [(0, "turn0"), (1, "turn1"), (2, "base1"), (3, "diag"), (5, "base2")]}.get(at)
    else:
        uses = {2: [(0, "diag"), (3, "turn0"), (5, "turn1"), (6, "base2")]}.get(at)
    uses = uses or [(1, "diag"), (5, "base2")]
    if last and k >= CHUNKS - 2:
        uses = [u for u in uses if "base" not in u[1]]
    if last and k >= TILE_CHUNKS:
        uses = [u for u in uses if "turn" not in u[1]]
    return uses


def group_rows(g):
    return ROWS if g < GROUPS - 1 else LAST_ROWS


def tower(nc, dense_t, ids, tables, pair_w, w1, w_top1a, w_top1b, b_top1, w_top2, b_top2, w_top3,
          select_const, ident_const, mask_const, out):
    ctx = ExitStack()
    with ctx:
        def sb(name, shape, dt=F32):
            return ctx.enter_context(nc.sbuf_tensor(name, shape, dt))

        def sem(name):
            return ctx.enter_context(nc.semaphore(name))

        w0_high = sb("w0_high", [ROWS, GROUPS, OUT], F32R)
        w0_low = sb("w0_low", [ROWS, GROUPS, OUT], F32R)
        w1_sb = sb("w1_sb", [OUT, FIELDS, OUT])
        top1a_sb = sb("top1a_sb", [P, 2, HID1])
        top1b_sb = sb("top1b_sb", [DENSE, HID1])
        top2_sb = sb("top2_sb", [P, HID1 // P, HID2])
        top3_sb = sb("top3_sb", [P, HID2 // P])
        bias1_sb = sb("bias1_sb", [P, HID1 // P])
        bias2_sb = sb("bias2_sb", [P, HID2 // P])
        dense_sb = sb("dense_sb", [DENSE, BATCH])
        select_raw = sb("select_raw", [ROWS, ROWS])
        select_sb = sb("select_sb", [ROWS, ROWS], BF16)
        ident_raw = sb("ident_raw", [P, P])
        ident_sb = sb("ident_sb", [P, P], BF16)
        ident_f32 = ident_raw
        mask_sb = sb("mask_sb", [P, SUB_SAMPLES])

        ids_sb = sb("ids_sb", [P, 2 * N_SUPER + 2, FIELDS], I32)
        idx_sb = sb("idx_sb", [P, 2, 2, FIELDS], I32)
        emb = sb("emb", [P, 2, 2, FIELDS * DIM])
        rest = sb("rest", [P, FIELDS * DIM])
        parts = sb("parts", [P, PARTS, FIELDS * DIM], BF16)
        cols = sb("cols", [ROWS, 2, TILE * DIM], BF16)
        slots = sb("slots", [ROWS, 2, SLOTS, COLS])
        pairs = sb("pairs", [ROWS, PAIR_BUFS, COLS])
        pairs_high = sb("pairs_high", [ROWS, Z_BUFS, COLS], F32R)
        pairs_low = sb("pairs_low", [ROWS, Z_BUFS, COLS], F32R)
        x1_turned = sb("x1_turned", [OUT, COLS])
        x1_sb = sb("x1_sb", [P, 2, SUBS * OUT])
        diag = sb("diag", [P, 2, SUBS, SUB_SAMPLES, MOMENTS])
        moments = sb("moments", [OUT, 2, MOMENTS, TILE])
        res_sb = sb("res_sb", [P, 2, SUPER])
        hid1_sb = sb("hid1_sb", [P, HID1 // P, SUPER])
        hid2_sb = sb("hid2_sb", [P, HID2 // P, SUPER])
        y_sb = sb("y_sb", [1, SUPER])
        waited = sb("waited", [1, 2])

        scratch = moments[:ROWS, 0].rearrange("p m b -> p (m b)")
        pair_raw = scratch[:, :GROUPS * 2 * OUT].rearrange("p (g x o) -> p g x o", g=GROUPS, x=2)
        w0_sb = scratch[:, GROUPS * 2 * OUT:GROUPS * 3 * OUT].rearrange("p (g o) -> p g o", g=GROUPS)

        cin1_ps = [ctx.enter_context(nc.psum_tensor(f"cin1_ps{i}", [OUT, COLS], F32)) for i in range(2)]
        x1_ps = ctx.enter_context(nc.psum_tensor("x1_ps", [P, SUBS * OUT], F32))
        cin2_ps = ctx.enter_context(nc.psum_tensor("cin2_ps", [OUT, TILE], F32))
        mom_ps = [ctx.enter_context(nc.psum_tensor(f"mom_ps{i}", [P, 512], F32)) for i in range(2)]
        misc_ps = ctx.enter_context(nc.psum_tensor("misc_ps", [P, 512], F32))
        top_ps = ctx.enter_context(nc.psum_tensor("top_ps", [P, 2, SUPER], F32))
        turn_ps = misc_ps[:, :].bitcast(BF16).rearrange("p (d b) -> p d b", b=TILE)
        MOM = SUB_SAMPLES * MOMENTS

        ids_loaded, idx_ready = sem("ids_loaded"), sem("idx_ready")
        gathered = [sem(f"gathered{t}") for t in range(2)]
        sel_loaded, pair_loaded, w1_loaded, top_loaded = (
            sem("sel_loaded"), sem("pair_loaded"), sem("w1_loaded"), sem("top_loaded"))
        waited_ready = sem("waited_ready")
        const_ready, ones_ready, w0_ready = sem("const_ready"), sem("ones_ready"), sem("w0_ready")
        high_done, rest_done, middle_done, split_done = (
            sem("high_done"), sem("rest_done"), sem("middle_done"), sem("split_done"))
        turned, cols_done = sem("turned"), sem("cols_done")
        base_sel, base_done = sem("base_sel"), sem("base_done")
        slot_loaded = [[sem(f"slot_loaded{b}_{u}") for u in range(SLOTS)] for b in range(2)]
        pairs_done, pairs_used = sem("pairs_done"), sem("pairs_used")
        pairs_rounded, pairs_split = sem("pairs_rounded"), sem("pairs_split")
        cin1_done, x1_turn, x1_done = sem("cin1_done"), sem("x1_turn"), sem("x1_done")
        diag_sel, diag_done = sem("diag_sel"), sem("diag_done")
        mom_sum, mom_done = sem("mom_sum"), sem("mom_done")
        cin2_sum, res_done = sem("cin2_sum"), sem("res_done")
        hid1_sum, hid1_done = sem("hid1_sum"), sem("hid1_done")
        hid2_sum, hid2_done = sem("hid2_sum"), sem("hid2_done")
        y_sum, y_done, y_stored = sem("y_sum"), sem("y_done"), sem("y_stored")

        def at_least(eng, semaphore, value):
            if not isinstance(value, int) or value > 0:
                eng.wait_ge(semaphore, value)

        def over_superblocks(eng, one):
            one(0)
            with eng.Fori(1, N_SUPER - 1) as sb_i:
                one(sb_i)
            one(N_SUPER - 1)

        def is_last(s):
            return isinstance(s, int) and s == N_SUPER - 1

        def chunk_range(s):
            return range(0 if isinstance(s, int) and s == 0 else 1, CHUNKS if is_last(s) else CHUNKS + 1)

        def top_step(s, k, g):
            if isinstance(s, int) and s == 0:
                return None
            return TOP_AT_LAST.get((k, g)) if is_last(s) else TOP_AT.get((k, g))

        block = ctx.enter_context(nc.Block())

        @block.sync
        def _(sp):
            def rotate(c, k):
                sp.wait_ge(base_done, c + 1)
                b = k % 2
                for u in range(1, SLOTS):
                    for j in range(PARTS):
                        if u < len(ROTATIONS[j]):
                            r = ROTATIONS[j][u]
                            sp.dma_start(slots[j * FIELDS:(j + 1) * FIELDS, b, u, :],
                                         slots[r:r + FIELDS, b, 0, :]).then_inc(slot_loaded[b][u], 16)

            sp.dma_start(ids_sb[:, :, :], ids).then_inc(ids_loaded, 16)
            sp.dma_start(select_raw[:, :], select_const).then_inc(sel_loaded, 16)
            sp.dma_start(ident_raw[:, :], ident_const).then_inc(sel_loaded, 16)
            sp.dma_start(mask_sb[:, :], mask_const).then_inc(sel_loaded, 16)
            sp.dma_start(pair_raw[:, :, :, :], pair_w).then_inc(pair_loaded, 16)
            sp.dma_start(w1_sb[:, :, :], w1).then_inc(w1_loaded, 16)
            for dst, src in ((top1a_sb, w_top1a), (top1b_sb, w_top1b), (top2_sb, w_top2),
                             (top3_sb, w_top3), (bias1_sb, b_top1), (bias2_sb, b_top2),
                             (dense_sb, dense_t)):
                sp.dma_start(dst.ap(), src).then_inc(top_loaded, 16)

            def store_y(s):
                at_least(sp, y_done, s + 1)
                sp.dma_start(out[bass.ds(s * SUPER, SUPER), :].rearrange("b o -> o b"),
                             y_sb[:, :]).then_inc(y_stored, 16)

            rotate(0, 0)
            rotate(1, 1)

            def superblock(s):
                start = isinstance(s, int) and s == 0
                for k in chunk_range(s):
                    if not (is_last(s) and k >= CHUNKS - 2):
                        rotate(CHUNKS * s + k + 2, k)
                if not start:
                    store_y(s - 1)

            over_superblocks(sp, superblock)
            store_y(N_SUPER - 1)
            sp.wait_ge(y_stored, 16 * N_SUPER)

        @block.gpsimd
        def _(pool):
            nc.gpsimd.memset(diag[:, 0], 0.0).then_inc(ones_ready, 1)
            nc.gpsimd.memset(diag[:, 1], 0.0).then_inc(ones_ready, 1)

            def superblock(s, b):
                for t in range(2):
                    for f in range(FIELDS):
                        pool.indirect_dma_start(
                            out=emb[:, b, t, f * DIM:(f + 1) * DIM], out_offset=None, in_=tables[f],
                            in_offset=bass.IndirectOffsetOnAxis(ap=idx_sb[:, b, t, f:f + 1], axis=0),
                        ).then_inc(gathered[t], 16)

            def before_next(s):
                for t in range(2):
                    pool.wait_ge(gathered[t], GATHERED * (s + 1))
                pool.wait_ge(idx_ready, s + 2)
                at_least(pool, rest_done, 2 * s)
                pool.wait_ge(waited_ready, s + 1)
                nc.gpsimd.tensor_tensor(waited[:, 1:2], waited[:, 0:1], waited[:, 0:1], ALU.add).then_inc(waited_ready, 1)

            nc.gpsimd.memset(waited[:, :], 0.0).then_inc(waited_ready, 1)
            pool.wait_ge(waited_ready, 1)
            pool.wait_ge(idx_ready, 1)
            superblock(0, 0)
            before_next(0)
            with pool.Fori(0, N_SUPER // 2 - 1) as pair:
                superblock(2 * pair + 1, 1)
                before_next(2 * pair + 1)
                superblock(2 * pair + 2, 0)
                before_next(2 * pair + 2)
            superblock(N_SUPER - 1, 1)

        @block.scalar
        def _(act):
            act.wait_ge(sel_loaded, 48)
            nc.scalar.copy(select_sb[:, :], select_raw[:, :]).then_inc(const_ready, 1)
            nc.scalar.copy(ident_sb[:, :], ident_raw[:, :]).then_inc(const_ready, 1)

            def high_part(s, t):
                act.wait_ge(gathered[t], GATHERED * (s + 1))
                at_least(act, turned, 2 * (2 * s + t))
                nc.scalar.copy(parts[:, 0, :], emb[:, s % 2, t, :]).then_inc(high_done, 1)

            def middle_part(s, t):
                act.wait_ge(rest_done, 2 * s + t + 1)
                nc.scalar.copy(parts[:, 1, :], rest[:, :]).then_inc(middle_done, 1)

            def store_cols(s, t, half):
                act.wait_ge(turned, 2 * (2 * s + t) + half + 1)
                dst = cols[:, t, :].rearrange("p (b d) -> p b d", d=DIM)[:, :, half * TURN:(half + 1) * TURN]
                nc.scalar.copy(dst, turn_ps[:ROWS].rearrange("p d b -> p b d")).then_inc(cols_done, 1)

            def store_base(c, k):
                act.wait_ge(base_sel, c + 1)
                at_least(act, pairs_done, GROUPS * (c - 1))
                nc.scalar.copy(slots[:, k % 2, 0, :], misc_ps[:ROWS, :]).then_inc(base_done, 1)

            def round_pairs(c, k, g):
                n, r, b, bp = GROUPS * c + g, group_rows(g), (GROUPS * k + g) % Z_BUFS, (GROUPS * k + g) % PAIR_BUFS
                act.wait_ge(pairs_done, n + 1)
                at_least(act, pairs_used, n + 1 - Z_BUFS)
                nc.scalar.copy(pairs_high[:r, b, :], pairs[:r, bp, :]).then_inc(pairs_rounded, 1)

            def store_cin1(c, k):
                act.wait_ge(pairs_used, GROUPS * (c + 1))
                at_least(act, x1_turn, c)
                nc.scalar.copy(x1_turned[:, :], cin1_ps[k % 2][:, :]).then_inc(cin1_done, 1)

            def store_x1(c, k):
                act.wait_ge(x1_turn, c + 1)
                at_least(act, mom_sum, SUBS * (c - 1))
                nc.scalar.copy(x1_sb[:, k % 2, :], x1_ps[:, :]).then_inc(x1_done, 1)

            def store_moments(c, k, j):
                act.wait_ge(mom_sum, SUBS * c + j + 1)
                first = (k % TILE_CHUNKS * SUBS + j) * SUB_SAMPLES
                nc.scalar.copy(moments[:, k // TILE_CHUNKS, :, first:first + SUB_SAMPLES],
                               mom_ps[j % 2][:, :MOM].rearrange("p (b m) -> p m b", m=MOMENTS)).then_inc(mom_done, 1)

            def store_results(s, t):
                act.wait_ge(cin2_sum, 2 * s + t + 1)
                at_t = slice(t * TILE, (t + 1) * TILE)
                nc.scalar.copy(res_sb[:, 0, at_t], moments[:, t, FIELDS, :]).then_inc(res_done, 1)
                nc.scalar.copy(res_sb[:, 1, at_t], cin2_ps[:, :]).then_inc(res_done, 1)

            def hidden1(s, half):
                act.wait_ge(hid1_sum, 2 * s + half + 1)
                for j in range(2):
                    o = 2 * half + j
                    nc.scalar.activation(hid1_sb[:, o, :], top_ps[:, j, :], ACT.Relu,
                                         bias=bias1_sb[:, o:o + 1]).then_inc(hid1_done, 1)

            def hidden2(s):
                act.wait_ge(hid2_sum, s + 1)
                for j in range(HID2 // P):
                    nc.scalar.activation(hid2_sb[:, j, :], top_ps[:, j, :], ACT.Relu,
                                         bias=bias2_sb[:, j:j + 1]).then_inc(hid2_done, 1)

            def store_result(s):
                act.wait_ge(y_sum, s + 1)
                at_least(act, y_stored, 16 * s)
                nc.scalar.copy(y_sb[:, :], top_ps[0:1, 0, :]).then_inc(y_done, 1)

            TOP_STEPS = [lambda s: hidden1(s, 0), lambda s: hidden1(s, 1), hidden2, store_result]

            def superblock(s):
                first = isinstance(s, int) and s == 0
                for k in chunk_range(s):
                    c = CHUNKS * s + k
                    before = not (first and k == 0)
                    split = not (is_last(s) and k >= TILE_CHUNKS)
                    s_t, t = s + (k // TILE_CHUNKS + 1) // 2, (k // TILE_CHUNKS + 1) % 2
                    uses = dict(shared_uses(k, first, is_last(s)))
                    k1 = (k - 1) % CHUNKS
                    if before:
                        store_cin1(c - 1, k1)
                    for g in range(GROUPS):
                        ka, ga = divmod(GROUPS * k + g + HIGH_AHEAD, GROUPS)
                        if not (is_last(s) and ka == CHUNKS):
                            round_pairs(CHUNKS * s + ka, ka, ga)
                        if g == TURN_X1_AT and before:
                            store_x1(c - 1, k1)
                        use = uses.get(g)
                        if use in ("base1", "base2"):
                            store_base(c + int(use[-1]), k + int(use[-1]))
                        elif use in ("turn0", "turn1"):
                            store_cols(s_t, t, int(use[-1]))
                        if g >= MOMENTS_AT and before:
                            store_moments(c - 1, k1, g - MOMENTS_AT)
                        if split and g == split_at(k, first, "high"):
                            high_part(s_t, t)
                        if split and g == split_at(k, first, "middle"):
                            middle_part(s_t, t)
                        if top_step(s, k, g) is not None:
                            TOP_STEPS[top_step(s, k, g)](s - 1)
                    if k == TILE_CHUNKS - 1 and not first:
                        store_results(s - 1, 1)
                    if k == 2 * TILE_CHUNKS - 1:
                        store_results(s, 0)

            act.wait_ge(w0_ready, 1)
            nc.scalar.copy(w0_high[:, :, :], w0_sb[:, :, :]).then_inc(w0_ready, 1)
            high_part(0, 0)
            middle_part(0, 0)
            store_cols(0, 0, 0)
            store_cols(0, 0, 1)
            store_base(0, 0)
            store_base(1, 1)
            for g in range(HIGH_AHEAD):
                round_pairs(0, 0, g)
            act.wait_ge(top_loaded, 7 * 16)
            over_superblocks(act, superblock)
            c = N_SUPER * CHUNKS - 1
            store_cin1(c, CHUNKS - 1)
            store_x1(c, CHUNKS - 1)
            for j in range(SUBS):
                store_moments(c, CHUNKS - 1, j)
            store_results(N_SUPER - 1, 1)
            for step in TOP_STEPS:
                step(N_SUPER - 1)

        @block.vector
        def _(dve):
            def rest_part(s, t):
                dve.wait_ge(high_done, 2 * s + t + 1)
                nc.vector.tensor_tensor(rest[:, :], emb[:, s % 2, t, :], parts[:, 0, :], ALU.subtract).then_inc(rest_done, 1)

            def low_part(s, t):
                dve.wait_ge(middle_done, 2 * s + t + 1)
                nc.vector.tensor_tensor(parts[:, 2, :], rest[:, :], parts[:, 1, :], ALU.subtract).then_inc(split_done, 1)

            def multiply(s, k, g):
                c = CHUNKS * s + k
                n, nk = GROUPS * c + g, GROUPS * k + g
                a, b = SLOT_PAIRS[g]
                if g == 0:
                    dve.wait_ge(base_done, c + 1)
                if a == 0:
                    dve.wait_ge(slot_loaded[k % 2][b], SLOT_DMAS[b] * (CHUNKS // 2 * s + k // 2 + 1))
                at_least(dve, pairs_split, n + 1 - PAIR_BUFS)
                r = group_rows(g)
                nc.vector.tensor_tensor(pairs[:r, nk % PAIR_BUFS, :], slots[:r, k % 2, a, :], slots[:r, k % 2, b, :],
                                        ALU.mult).then_inc(pairs_done, 1)

            def low_pairs(c, k, g):
                n, r, b, bp = GROUPS * c + g, group_rows(g), (GROUPS * k + g) % Z_BUFS, (GROUPS * k + g) % PAIR_BUFS
                dve.wait_ge(pairs_rounded, n + 1)
                at_least(dve, pairs_used, n + 1 - Z_BUFS)
                nc.vector.tensor_tensor(pairs_low[:r, b, :], pairs[:r, bp, :], pairs_high[:r, b, :].bitcast(F32),
                                        ALU.subtract).then_inc(pairs_split, 1)

            def fill_diagonal(c, k):
                dve.wait_ge(diag_sel, c + 1)
                at_least(dve, mom_sum, SUBS * (c - 1))
                fields = misc_ps[:, :SUBS * FIELDS].rearrange("p (j m) -> p j m", m=FIELDS)
                shape = [P, SUBS, SUB_SAMPLES, FIELDS]
                nc.vector.tensor_tensor(
                    diag[:, k % 2, :, :, 0:FIELDS], fields.unsqueeze(2).to_broadcast(shape),
                    mask_sb[:, :].unsqueeze(1).unsqueeze(3).to_broadcast(shape), ALU.mult,
                ).then_inc(diag_done, 1)

            def take_indices(s, b):
                nc.vector.tensor_copy(idx_sb[:, b], ids_sb[:, bass.ds(2 * s, 2), :]).then_inc(idx_ready, 1)

            dve.wait_ge(ids_loaded, 16)
            take_indices(0, 0)
            take_indices(1, 1)
            dve.wait_ge(ones_ready, 2)
            dve.wait_ge(sel_loaded, 48)
            for b in range(2):
                nc.vector.tensor_copy(diag[:, b, :, :, FIELDS],
                                      mask_sb[:, :].unsqueeze(1).to_broadcast([P, SUBS, SUB_SAMPLES])).then_inc(ones_ready, 1)
            dve.wait_ge(pair_loaded, 16)
            nc.vector.tensor_tensor(w0_sb[:, :, :], pair_raw[:, :, 0, :], pair_raw[:, :, 1, :], ALU.add).then_inc(w0_ready, 1)
            dve.wait_ge(w0_ready, 2)
            nc.vector.tensor_tensor(w0_low[:, :, :], w0_sb[:, :, :], w0_high[:, :, :].bitcast(F32),
                                    ALU.subtract).then_inc(w0_ready, 1)
            rest_part(0, 0)
            low_part(0, 0)

            def superblock(s):
                first = isinstance(s, int) and s == 0
                for k in chunk_range(s):
                    split = not (is_last(s) and k >= TILE_CHUNKS)
                    s_t, t = s + (k // TILE_CHUNKS + 1) // 2, (k // TILE_CHUNKS + 1) % 2
                    c = CHUNKS * s + k
                    for g in range(GROUPS):
                        multiply(s, k, g)
                        if g >= LOW_LAG:
                            low_pairs(c, k, g - LOW_LAG)
                        elif not (first and k == 0):
                            low_pairs(c - 1, (k - 1) % CHUNKS, GROUPS + g - LOW_LAG)
                        if split and g == split_at(k, first, "rest"):
                            rest_part(s_t, t)
                        if g == (DIAG_EARLY if k % TILE_CHUNKS == 2 else DIAG_AT):
                            fill_diagonal(c, k)
                        if split and g == split_at(k, first, "low"):
                            low_part(s_t, t)
                    if k == 3 and not is_last(s):
                        for tile in range(2):
                            dve.wait_ge(gathered[tile], GATHERED * (s + 1))
                        take_indices(s + 2, s % 2)

            over_superblocks(dve, superblock)
            for g in range(GROUPS - LOW_LAG, GROUPS):
                low_pairs(N_SUPER * CHUNKS - 1, CHUNKS - 1, g)

        @block.tensor
        def _(pe):
            mm = nc.tensor.matmul

            def turn(s, t, half):
                pe.wait_ge(split_done, 2 * s + t + 1)
                by_dim = parts[:, :, :].rearrange("p a (m d) -> p d (a m)", d=DIM)
                for i in range(TURN):
                    last = nc.tensor.transpose(turn_ps[:ROWS, i, :], by_dim[:, half * TURN + i, :], ident_sb[:, :])
                last.then_inc(turned, 1)

            def column_range(k):
                first = k % TILE_CHUNKS * COLS
                return cols[:, k // TILE_CHUNKS % 2, first:first + COLS]

            def select_base(c, k):
                mm(misc_ps[:ROWS, :], select_sb[:, :], column_range(k),
                   start=True, stop=True).then_inc(base_sel, 1)

            def select_diagonal(k):
                for j in range(SUBS):
                    last = mm(misc_ps[:, j * FIELDS:(j + 1) * FIELDS], column_range(k)[:, j * P:(j + 1) * P],
                              select_sb[:, 0:FIELDS], start=True, stop=True)
                last.then_inc(diag_sel, 1)

            def cin1(c, k, g):
                r, b = group_rows(g), (GROUPS * k + g) % Z_BUFS
                pe.wait_ge(pairs_split, GROUPS * c + g + 1)
                if g == 0:
                    at_least(pe, cin1_done, c - 1)
                for weights, products in ((w0_high, pairs_high), (w0_low, pairs_high), (w0_high, pairs_low)):
                    last = mm(cin1_ps[k % 2][:, :], weights[:r, g, :], products[:r, b, :],
                              start=(g == 0 and weights is w0_high and products is pairs_high),
                              stop=(g == GROUPS - 1 and products is pairs_low))
                last.then_inc(pairs_used, 1)

            def turn_x1(c):
                pe.wait_ge(cin1_done, c + 1)
                at_least(pe, x1_done, c)
                for j in range(SUBS):
                    last = nc.tensor.transpose(x1_ps[:, j * OUT:(j + 1) * OUT], x1_turned[:, j * P:(j + 1) * P],
                                               ident_f32[:, :])
                last.then_inc(x1_turn, 1)

            def sum_moments(c, k, j):
                if j == 0:
                    pe.wait_ge(x1_done, c + 1)
                    pe.wait_ge(diag_done, c + 1)
                at_least(pe, mom_done, SUBS * c + j - 1)
                mm(mom_ps[j % 2][:, :MOM], x1_sb[:, k % 2, j * OUT:(j + 1) * OUT], diag[:, k % 2, j, :, :],
                   start=True, stop=True).then_inc(mom_sum, 1)

            def cin2(s, t, fields):
                for m in fields:
                    if m == 0:
                        pe.wait_ge(mom_done, SUBS * TILE_CHUNKS * (2 * s + t + 1))
                        at_least(pe, res_done, 2 * (2 * s + t))
                    last = mm(cin2_ps[:, :], w1_sb[:, m, :], moments[:, t, m, :], start=(m == 0), stop=(m == FIELDS - 1))
                    if m == FIELDS - 1:
                        last.then_inc(cin2_sum, 1)

            def hidden1(s, half):
                if half:
                    pe.wait_ge(hid1_done, 4 * s + 2)
                else:
                    pe.wait_ge(res_done, 4 * (s + 1))
                    at_least(pe, y_done, s)
                for j in range(2):
                    o = (2 * half + j) * P
                    for i in range(2):
                        mm(top_ps[:, j, :], top1a_sb[:, i, o:o + P], res_sb[:, i, :], start=(i == 0), stop=False)
                    last = mm(top_ps[:, j, :], top1b_sb[:, o:o + P], dense_sb[:, bass.ds(s * SUPER, SUPER)],
                              start=False, stop=True)
                last.then_inc(hid1_sum, 1)

            def hidden2(s):
                pe.wait_ge(hid1_done, 4 * (s + 1))
                for j in range(HID2 // P):
                    for i in range(HID1 // P):
                        last = mm(top_ps[:, j, :], top2_sb[:, i, j * P:(j + 1) * P], hid1_sb[:, i, :],
                                  start=(i == 0), stop=(i == HID1 // P - 1))
                last.then_inc(hid2_sum, 1)

            def result(s):
                pe.wait_ge(hid2_done, 2 * (s + 1))
                for i in range(HID2 // P):
                    last = mm(top_ps[0:1, 0, :], top3_sb[:, i:i + 1], hid2_sb[:, i, :],
                              start=(i == 0), stop=(i == HID2 // P - 1))
                last.then_inc(y_sum, 1)

            TOP_STEPS = [lambda s: hidden1(s, 0), lambda s: hidden1(s, 1), hidden2, result]

            pe.wait_ge(const_ready, 2)
            turn(0, 0, 0)
            pe.wait_ge(cols_done, 1)
            turn(0, 0, 1)
            pe.wait_ge(cols_done, 2)
            select_base(0, 0)
            pe.wait_ge(base_done, 1)
            select_base(1, 1)
            pe.wait_ge(w0_ready, 3)
            pe.wait_ge(ones_ready, 4)
            pe.wait_ge(w1_loaded, 16)
            pe.wait_ge(top_loaded, 7 * 16)

            def shared_use(s, k, use):
                first, last = isinstance(s, int) and s == 0, is_last(s)
                uses = [u for _, u in shared_uses(k, first, last)]
                c = CHUNKS * s + k
                if use != uses[0]:
                    prior, kp = uses[uses.index(use) - 1], k
                elif first and k == 0:
                    prior, kp = "base2", -1
                else:
                    prior, kp = shared_uses((k - 1) % CHUNKS, first, last and k > 0)[-1][1], k - 1
                if "base" in prior:
                    pe.wait_ge(base_done, c - k + kp + int(prior[-1]) + 1)
                elif prior == "diag":
                    pe.wait_ge(diag_done, c - k + kp + 1)
                else:
                    pe.wait_ge(cols_done, 2 * (2 * s + kp // TILE_CHUNKS + 1) + int(prior[-1]) + 1)
                if "base" in use:
                    ahead = k + int(use[-1])
                    if ahead % TILE_CHUNKS == 0:
                        pe.wait_ge(cols_done, 2 * (2 * s + ahead // TILE_CHUNKS + 1))
                    select_base(c - k + ahead, ahead % CHUNKS)
                elif use == "diag":
                    select_diagonal(k)
                else:
                    tile = k // TILE_CHUNKS + 1
                    turn(s + tile // 2, tile % 2, int(use[-1]))

            def superblock(s):
                first = isinstance(s, int) and s == 0
                for k in chunk_range(s):
                    c = CHUNKS * s + k
                    before = not (first and k == 0)
                    uses = dict(shared_uses(k, first, is_last(s)))
                    for g in range(GROUPS):
                        if g in uses:
                            shared_use(s, k, uses[g])
                        cin1(c, k, g)
                        if g == TURN_X1_AT and before:
                            turn_x1(c - 1)
                        if g >= MOMENTS_AT and before:
                            sum_moments(c - 1, (k - 1) % CHUNKS, g - MOMENTS_AT)
                        slot = (k % TILE_CHUNKS - 1) * GROUPS + g - CIN2_AT
                        if slot >= 0 and not (first and k < TILE_CHUNKS):
                            fields = range(slot * CIN2_STEP, min(FIELDS, (slot + 1) * CIN2_STEP))
                            if k < TILE_CHUNKS:
                                cin2(s - 1, 1, fields)
                            else:
                                cin2(s, 0, fields)
                        if top_step(s, k, g) is not None:
                            TOP_STEPS[top_step(s, k, g)](s - 1)

            over_superblocks(pe, superblock)
            c = N_SUPER * CHUNKS - 1
            turn_x1(c)
            for j in range(SUBS):
                sum_moments(c, CHUNKS - 1, j)
            cin2(N_SUPER - 1, 1, range(FIELDS))
            for step in TOP_STEPS:
                step(N_SUPER - 1)


def select_constant():
    rows = np.arange(ROWS) % FIELDS
    return (rows[:, None] == rows[None, :]).astype(np.float32)


def pair_rows():
    j, m = np.divmod(np.arange(ROWS), FIELDS)
    turn = np.array([[r[u] if u < len(r) else -1 for u in range(SLOTS)] for r in ROTATIONS])
    a, b = np.array(SLOT_PAIRS).T
    x, y = ((m[:, None] + turn[j][:, i]) % FIELDS for i in (a, b))
    return x * FIELDS + y, y * FIELDS + x, x == y, (turn[j][:, a] < 0) | (turn[j][:, b] < 0)


def kernel(**inputs):
    import concourse.bacc as bacc
    from concourse.bass_utils import run_bass_kernel_spmd

    a = {k: np.ascontiguousarray(v) for k, v in inputs.items()}
    w0, rows = a["L0_rec_W0"], pair_rows()
    pair_w = np.stack([w0[rows[0]], w0[rows[1]]], axis=2)
    pair_w[rows[2], 1] = 0
    pair_w[rows[3]] = 0
    arrays = {
        "dense_t": a["dense_ctx"].T,
        "ids": np.pad(a["ids"], ((0, SUPER), (0, 0))).reshape(-1, TILE, FIELDS).transpose(1, 0, 2),
        **{f"tbl_{f}": a[f"tbl_{f}"] for f in range(FIELDS)},
        "pair_w": pair_w,
        "w1": a["L0_rec_W1"].reshape(FIELDS, OUT, OUT).transpose(1, 0, 2),
        "w_top1a": a["W_top1"][:2 * P].reshape(2, P, HID1).transpose(1, 0, 2),
        "w_top1b": a["W_top1"][2 * P:],
        "b_top1": a["b_top1"].reshape(HID1 // P, P).T,
        "w_top2": a["W_top2"].reshape(HID1 // P, P, HID2).transpose(1, 0, 2),
        "b_top2": a["b_top2"].reshape(HID2 // P, P).T,
        "w_top3": a["W_top3"][:, 0].reshape(HID2 // P, P).T,
        "select_const": select_constant(),
        "ident_const": np.eye(P, dtype=np.float32),
        "mask_const": (np.arange(P)[:, None] // DIM == np.arange(SUB_SAMPLES)).astype(np.float32),
    }
    arrays = {f"in_{k}": np.ascontiguousarray(v) for k, v in arrays.items()}
    nc = bacc.Bacc("TRN2", target_bir_lowering=False, num_devices=1)
    ap = {k[3:]: nc.dram_tensor(k, v.shape, mybir.dt.from_np(v.dtype), kind="ExternalInput").ap()
          for k, v in arrays.items()}
    out = nc.dram_tensor("out_y", (BATCH, 1), F32, kind="ExternalOutput").ap()
    tower(nc, ap["dense_t"], ap["ids"], [ap[f"tbl_{f}"] for f in range(FIELDS)], ap["pair_w"], ap["w1"],
          ap["w_top1a"], ap["w_top1b"], ap["b_top1"], ap["w_top2"], ap["b_top2"], ap["w_top3"],
          ap["select_const"], ap["ident_const"], ap["mask_const"], out)
    r = run_bass_kernel_spmd(nc, [arrays], core_ids=[0])
    return r.results[0]["out_y"]
```

```python
import numpy as np
import concourse.bass as bass
from concourse import mybir
from contextlib import ExitStack

F32, F32R, BF16, I32 = mybir.dt.float32, mybir.dt.float32r, mybir.dt.bfloat16, mybir.dt.int32
ACT, ALU = mybir.ActivationFunctionType, mybir.AluOpType

BATCH, FIELDS, DIM = 2048, 39, 16
OUT = 128
DENSE, HID1, HID2 = 16, 512, 256
P = 128
TILE = 128
SUPER = 256
CHUNK = 32
COLS = CHUNK * DIM
N_SUPER = BATCH // SUPER
CHUNKS = SUPER // CHUNK
TILE_CHUNKS = TILE // CHUNK
PARTS = 3
ROWS = PARTS * FIELDS
ROTATIONS = ((0, 1, 6, 31, 0), (0, 2, 12, 23, 13), (0, 3, 7, 22, 0))
SLOTS = 5
SLOT_DMAS = [16 * sum(r[u] > 0 for r in ROTATIONS) for u in range(SLOTS)]
SLOT_PAIRS = ((0, 1), (0, 2), (1, 2), (0, 3), (1, 3), (2, 3), (0, 4))
GROUPS = len(SLOT_PAIRS)
LAST, LAST_ROWS = GROUPS - 1, 2 * FIELDS
WEIGHTS = GROUPS + 1
SUBS = COLS // P
SUB_SAMPLES = P // DIM
DENSE_PAIRS = ((0, 0), (0, 1), (1, 0), (0, 2), (2, 0), (1, 1), (1, 2), (2, 1))
MOMENTS = FIELDS + 1
TURN = 4
QUARTERS = DIM // TURN
PAIR_BUFS = 4
HIGH_AHEAD = 4
LOW_LAG = 2
MOMENTS_AT = 3
TURN_X1_AT = 1
DIAG_AT, DIAG_EARLY = 6, 5
TOP_AT = {(4, 1): 0, (4, 4): 1, (CHUNKS, 1): 2, (CHUNKS, 5): 3}
TOP_AT_LAST = {(4, 1): 0, (4, 4): 1, (6, 1): 2, (6, 5): 3}
TURNS_AT = 3
REPEAT_AT = 6
CIN2_AT = 1
CIN2_STEP = -(-FIELDS // (GROUPS * (TILE_CHUNKS - 1) - CIN2_AT))
GATHERED = FIELDS * 16


def in_first_tile(k, start):
    return start and k < TILE_CHUNKS


def shared_uses(k, start, last):
    at = k % TILE_CHUNKS
    if in_first_tile(k, start):
        if at == 3:
            return [(0, "turn0"), (1, "turn1"), (2, "turn2"), (3, "turn3"), (4, "diag")]
    elif at == 2:
        turns = [] if last and k >= TILE_CHUNKS else [(g, f"turn{g - TURNS_AT}") for g in range(TURNS_AT, GROUPS)]
        return [(0, "diag")] + turns
    return [(1, "diag")]


def taken(k, g, start, last):
    quarter = GROUPS * (k % TILE_CHUNKS - 2) + g + (-3 if in_first_tile(k, start) else 1)
    return quarter if 0 <= quarter < QUARTERS and not (last and k >= TILE_CHUNKS) else None


def rotated(k, start, last):
    if last and k >= CHUNKS - 2:
        return []
    if in_first_tile(k, start) and k >= 2:
        return [[], [1, 2]][k - 2]
    return [2]


def tower(nc, dense_t, ids, tables, pair_w, w1, w_top1a, w_top1b, b_top1, w_top2, b_top2, w_top3,
          ident_const, mask_const, out):
    ctx = ExitStack()
    with ctx:
        def sb(name, shape, dt=F32):
            return ctx.enter_context(nc.sbuf_tensor(name, shape, dt))

        def sem(name):
            return ctx.enter_context(nc.semaphore(name))

        w0_high = sb("w0_high", [ROWS, WEIGHTS, OUT], F32R)
        w0_low = sb("w0_low", [ROWS, WEIGHTS, OUT], F32R)
        w1_sb = sb("w1_sb", [OUT, FIELDS, OUT])
        top1a_sb = sb("top1a_sb", [P, 2, HID1])
        top2_sb = sb("top2_sb", [P, HID1 // P, HID2])
        top3_sb = sb("top3_sb", [P, HID2 // P])
        bias1_sb = sb("bias1_sb", [P, HID1 // P])
        bias2_sb = sb("bias2_sb", [P, HID2 // P])
        dense_sb = sb("dense_sb", [P, BATCH + HID1], BF16)
        ident_sb = sb("ident_sb", [P, P])
        mask_sb = sb("mask_sb", [P, SUB_SAMPLES])

        ids_sb = sb("ids_sb", [P, 2 * N_SUPER + 2, FIELDS], I32)
        idx_sb = sb("idx_sb", [P, 2, 2, FIELDS], I32)
        emb = sb("emb", [P, 2, 2, FIELDS * DIM])
        rows = sb("rows", [P, DIM, PARTS, FIELDS])
        cols = sb("cols", [ROWS, 2, TILE * DIM])
        slots = sb("slots", [ROWS, 2, SLOTS - 1, COLS])
        pairs = sb("pairs", [ROWS, PAIR_BUFS, COLS])
        pairs_high = sb("pairs_high", [ROWS, GROUPS, COLS], F32R)
        pairs_low = sb("pairs_low", [ROWS, GROUPS, COLS], F32R)
        x1_turned = sb("x1_turned", [OUT, COLS])
        x1_sb = sb("x1_sb", [P, 2, SUBS * OUT])
        diag = sb("diag", [P, 2, SUBS, SUB_SAMPLES, MOMENTS])
        moments = sb("moments", [OUT, 2, MOMENTS, TILE])
        res_sb = sb("res_sb", [P, 2, SUPER])
        hid1_sb = sb("hid1_sb", [P, HID1 // P, SUPER])
        hid2_sb = sb("hid2_sb", [P, HID2 // P, SUPER])
        y_sb = sb("y_sb", [1, SUPER])
        waited = sb("waited", [1, 2])

        scratch = moments[:ROWS, 0].rearrange("p m b -> p (m b)")
        pair_raw = scratch[:, :WEIGHTS * 2 * OUT].rearrange("p (g x o) -> p g x o", g=WEIGHTS, x=2)
        dense_raw, dense_rest = (moments[:DENSE, 1].rearrange("p m b -> p (m b)")[:, i * (BATCH + HID1):
                                 (i + 1) * (BATCH + HID1)] for i in range(2))
        dense_parts = cols[:DENSE].rearrange("p t c -> p (t c)").bitcast(BF16)[:, :PARTS * (BATCH + HID1)].rearrange(
            "p (a c) -> p a c", a=PARTS)
        w0_sb = scratch[:, WEIGHTS * 2 * OUT:WEIGHTS * 3 * OUT].rearrange("p (g o) -> p g o", g=WEIGHTS)

        cin1_ps = [ctx.enter_context(nc.psum_tensor(f"cin1_ps{i}", [OUT, COLS], F32)) for i in range(2)]
        x1_ps = ctx.enter_context(nc.psum_tensor("x1_ps", [P, SUBS * OUT], F32))
        cin2_ps = ctx.enter_context(nc.psum_tensor("cin2_ps", [OUT, TILE], F32))
        mom_ps = [ctx.enter_context(nc.psum_tensor(f"mom_ps{i}", [P, 512], F32)) for i in range(2)]
        misc_ps = ctx.enter_context(nc.psum_tensor("misc_ps", [P, 512], F32))
        top_ps = ctx.enter_context(nc.psum_tensor("top_ps", [P, 2, SUPER], F32))
        turn_ps = misc_ps[:, :].rearrange("p (d b) -> p d b", b=TILE)
        first_turn_ps = [bank[:, :].rearrange("p (d b) -> p d b", b=TILE) for bank in (cin1_ps[1], x1_ps, *mom_ps)]
        MOM = SUB_SAMPLES * MOMENTS
        top_halves = [top_ps[:, j, :] for j in range(2)]
        end_hidden1 = [top_ps[:, 0, :], cin1_ps[0][:, :SUPER], cin1_ps[1][:, :SUPER], x1_ps[:, :SUPER]]
        end_hidden2 = [mom[:, :SUPER] for mom in mom_ps]

        ids_loaded, idx_ready = sem("ids_loaded"), sem("idx_ready")
        gathered = [sem(f"gathered{t}") for t in range(2)]
        const_loaded, pair_loaded, w1_loaded, top_loaded = (
            sem("const_loaded"), sem("pair_loaded"), sem("w1_loaded"), sem("top_loaded"))
        waited_ready = sem("waited_ready")
        dense_loaded, dense_split, dense_ready = sem("dense_loaded"), sem("dense_split"), sem("dense_ready")
        ones_ready, w0_ready = sem("ones_ready"), sem("w0_ready")
        rows_done = sem("rows_done")
        turned, cols_done = sem("turned"), sem("cols_done")
        base_repeated = sem("base_repeated")
        slot_loaded = [[sem(f"slot_loaded{b}_{u}") for u in range(SLOTS)] for b in range(2)]
        pairs_done, pairs_used = sem("pairs_done"), sem("pairs_used")
        pairs_rounded, pairs_split, high_copied = sem("pairs_rounded"), sem("pairs_split"), sem("high_copied")
        cin1_done, x1_turn, x1_done = sem("cin1_done"), sem("x1_turn"), sem("x1_done")
        diag_turned, diag_done = sem("diag_turned"), sem("diag_done")
        mom_sum, mom_done = sem("mom_sum"), sem("mom_done")
        cin2_sum, res_done = sem("cin2_sum"), sem("res_done")
        hid1_sum, hid1_done = sem("hid1_sum"), sem("hid1_done")
        hid2_sum, hid2_done = sem("hid2_sum"), sem("hid2_done")
        y_sum, y_done, y_stored = sem("y_sum"), sem("y_done"), sem("y_stored")

        def at_least(eng, semaphore, value):
            if not isinstance(value, int) or value > 0:
                eng.wait_ge(semaphore, value)

        def over_superblocks(eng, one):
            one(0)
            with eng.Fori(1, N_SUPER - 1) as sb_i:
                one(sb_i)
            one(N_SUPER - 1)

        def is_last(s):
            return isinstance(s, int) and s == N_SUPER - 1

        def base_of(k):
            first = k % TILE_CHUNKS * COLS
            return cols[:, k // TILE_CHUNKS % 2, first:first + COLS]

        def cols_of(s, k):
            return QUARTERS * (2 * s + k // TILE_CHUNKS + 1)

        def chunk_range(s):
            return range(0 if isinstance(s, int) and s == 0 else 1, CHUNKS if is_last(s) else CHUNKS + 1)

        def top_step(s, k, g):
            if isinstance(s, int) and s == 0:
                return None
            return TOP_AT_LAST.get((k, g)) if is_last(s) else TOP_AT.get((k, g))

        block = ctx.enter_context(nc.Block())

        @block.sync
        def _(sp):
            def rotate(s, k):
                c, b = CHUNKS * s + k, k % 2
                sp.wait_ge(cols_done, cols_of(s, k))
                at_least(sp, pairs_done, GROUPS * (c - 1))
                for u in range(1, SLOTS):
                    if u == SLOTS - 1:
                        sp.wait_ge(base_repeated, c + 1)
                    for j in range(PARTS):
                        r = ROTATIONS[j][u]
                        if r == 0:
                            continue
                        sp.dma_start(slots[j * FIELDS:(j + 1) * FIELDS, b, u - 1, :],
                                     base_of(k)[r:r + FIELDS, :]).then_inc(slot_loaded[b][u], 16)

            def repeat_high(c):
                sp.wait_ge(pairs_rounded, GROUPS * (c + 1))
                sp.dma_start(pairs_low[LAST_ROWS:ROWS, LAST, :].bitcast(F32),
                             pairs_high[FIELDS:LAST_ROWS, LAST, :].bitcast(F32)).then_inc(high_copied, 16)

            sp.dma_start(ids_sb[:, :, :], ids).then_inc(ids_loaded, 16)
            sp.dma_start(ident_sb[:, :], ident_const).then_inc(const_loaded, 16)
            sp.dma_start(mask_sb[:, :], mask_const).then_inc(const_loaded, 16)
            sp.dma_start(pair_raw[:, :, :, :], pair_w).then_inc(pair_loaded, 16)
            sp.dma_start(dense_raw[:, :BATCH], dense_t).then_inc(dense_loaded, 16)
            sp.dma_start(dense_raw[:, BATCH:], w_top1b).then_inc(dense_loaded, 16)
            sp.dma_start(w1_sb[:, :, :], w1).then_inc(w1_loaded, 16)
            for dst, src in ((top1a_sb, w_top1a), (top2_sb, w_top2), (top3_sb, w_top3),
                             (bias1_sb, b_top1), (bias2_sb, b_top2)):
                sp.dma_start(dst.ap(), src).then_inc(top_loaded, 16)
            sp.wait_ge(dense_split, 4)
            for i, (part, weight_part) in enumerate(DENSE_PAIRS):
                block_rows = dense_sb[i * DENSE:(i + 1) * DENSE, :]
                sp.dma_start(block_rows[:, :BATCH], dense_parts[:, part, :BATCH]).then_inc(dense_ready, 16)
                sp.dma_start(block_rows[:, BATCH:], dense_parts[:, weight_part, BATCH:]).then_inc(dense_ready, 16)

            def store_y(s):
                at_least(sp, y_done, s + 1)
                sp.dma_start(out[bass.ds(s * SUPER, SUPER), :].rearrange("b o -> o b"),
                             y_sb[:, :]).then_inc(y_stored, 16)

            rotate(0, 0)
            rotate(0, 1)

            def superblock(s):
                start = isinstance(s, int) and s == 0
                for k in chunk_range(s):
                    repeat_high(CHUNKS * s + k)
                    for ahead in rotated(k, start, is_last(s)):
                        rotate(s, k + ahead)
                if not start:
                    store_y(s - 1)

            over_superblocks(sp, superblock)
            store_y(N_SUPER - 1)
            sp.wait_ge(y_stored, 16 * N_SUPER)

        @block.gpsimd
        def _(pool):
            nc.gpsimd.memset(diag[:, 0], 0.0).then_inc(ones_ready, 1)
            nc.gpsimd.memset(diag[:, 1], 0.0).then_inc(ones_ready, 1)

            def superblock(s, b):
                for t in range(2):
                    for f in range(FIELDS):
                        pool.indirect_dma_start(
                            out=emb[:, b, t, f * DIM:(f + 1) * DIM], out_offset=None, in_=tables[f],
                            in_offset=bass.IndirectOffsetOnAxis(ap=idx_sb[:, b, t, f:f + 1], axis=0),
                        ).then_inc(gathered[t], 16)

            def before_next(s):
                for t in range(2):
                    pool.wait_ge(gathered[t], GATHERED * (s + 1))
                pool.wait_ge(idx_ready, s + 2)
                at_least(pool, rows_done, 2 * QUARTERS * s)
                pool.wait_ge(waited_ready, s + 1)
                nc.gpsimd.tensor_tensor(waited[:, 1:2], waited[:, 0:1], waited[:, 0:1], ALU.add).then_inc(waited_ready, 1)

            nc.gpsimd.memset(waited[:, :], 0.0).then_inc(waited_ready, 1)
            pool.wait_ge(waited_ready, 1)
            pool.wait_ge(idx_ready, 1)
            superblock(0, 0)
            before_next(0)
            with pool.Fori(0, N_SUPER // 2 - 1) as pair:
                superblock(2 * pair + 1, 1)
                before_next(2 * pair + 1)
                superblock(2 * pair + 2, 0)
                before_next(2 * pair + 2)
            superblock(N_SUPER - 1, 1)

        @block.scalar
        def _(act):
            def repeat_rows(s, t, quarter):
                act.wait_ge(gathered[t], GATHERED * (s + 1))
                at_least(act, turned, QUARTERS * (2 * s + t - 1) + quarter + 1)
                by_dim = emb[:, s % 2, t, :].rearrange("p (m d) -> p d m", d=DIM)[:, quarter * TURN:(quarter + 1) * TURN]
                nc.scalar.copy(rows[:, quarter * TURN:(quarter + 1) * TURN],
                               by_dim.unsqueeze(2).to_broadcast([P, TURN, PARTS, FIELDS])).then_inc(rows_done, 1)

            def store_cols(s, t, quarter, turned_ps):
                tile = 2 * s + t
                act.wait_ge(turned, QUARTERS * tile + quarter + 1)
                at_least(act, pairs_done, GROUPS * TILE_CHUNKS * (tile - 1))
                dst = cols[:, t, :].rearrange("p (b d) -> p b d", d=DIM)[:, :, quarter * TURN:(quarter + 1) * TURN]
                nc.scalar.copy(dst, turned_ps[:ROWS].rearrange("p d b -> p b d")).then_inc(cols_done, 1)

            def repeat_base(s, k):
                act.wait_ge(cols_done, cols_of(s, k))
                at_least(act, pairs_done, GROUPS * (CHUNKS * s + k - 1))
                nc.scalar.copy(slots[:, k % 2, SLOTS - 2, :], base_of(k)).then_inc(base_repeated, 1)

            def round_pairs(c, k, g):
                n, bp = GROUPS * c + g, (GROUPS * k + g) % PAIR_BUFS
                act.wait_ge(pairs_done, n + 1)
                at_least(act, pairs_used, n + 1 - GROUPS)
                nc.scalar.copy(pairs_high[:, g, :], pairs[:, bp, :]).then_inc(pairs_rounded, 1)

            def store_cin1(c, k):
                act.wait_ge(pairs_used, GROUPS * (c + 1))
                at_least(act, x1_turn, c)
                nc.scalar.copy(x1_turned[:, :], cin1_ps[k % 2][:, :]).then_inc(cin1_done, 1)

            def store_x1(c, k):
                act.wait_ge(x1_turn, c + 1)
                at_least(act, mom_sum, SUBS * (c - 1))
                nc.scalar.copy(x1_sb[:, k % 2, :], x1_ps[:, :]).then_inc(x1_done, 1)

            def store_moments(c, k, j):
                act.wait_ge(mom_sum, SUBS * c + j + 1)
                first = (k % TILE_CHUNKS * SUBS + j) * SUB_SAMPLES
                nc.scalar.copy(moments[:, k // TILE_CHUNKS, :, first:first + SUB_SAMPLES],
                               mom_ps[j % 2][:, :MOM].rearrange("p (b m) -> p m b", m=MOMENTS)).then_inc(mom_done, 1)

            def store_sums(s, t):
                act.wait_ge(mom_done, SUBS * TILE_CHUNKS * (2 * s + t + 1))
                nc.scalar.copy(res_sb[:, 0, t * TILE:(t + 1) * TILE], moments[:, t, FIELDS, :]).then_inc(res_done, 1)

            def store_cin2(s, t):
                act.wait_ge(cin2_sum, 2 * s + t + 1)
                nc.scalar.copy(res_sb[:, 1, t * TILE:(t + 1) * TILE], cin2_ps[:, :]).then_inc(res_done, 1)

            def hidden1(s, half, sums):
                act.wait_ge(hid1_sum, 2 * s + half + 1)
                for j in range(2):
                    o = 2 * half + j
                    nc.scalar.activation(hid1_sb[:, o, :], sums[j], ACT.Relu,
                                         bias=bias1_sb[:, o:o + 1]).then_inc(hid1_done, 1)

            def hidden2(s, sums):
                act.wait_ge(hid2_sum, s + 1)
                for j in range(HID2 // P):
                    nc.scalar.activation(hid2_sb[:, j, :], sums[j], ACT.Relu,
                                         bias=bias2_sb[:, j:j + 1]).then_inc(hid2_done, 1)

            def store_result(s):
                act.wait_ge(y_sum, s + 1)
                at_least(act, y_stored, 16 * s)
                nc.scalar.copy(y_sb[:, :], top_ps[0:1, 0, :]).then_inc(y_done, 1)

            TOP_STEPS = [lambda s: hidden1(s, 0, top_halves), lambda s: hidden1(s, 1, top_halves),
                         lambda s: hidden2(s, top_halves), store_result]

            def superblock(s):
                first = isinstance(s, int) and s == 0
                for k in chunk_range(s):
                    c = CHUNKS * s + k
                    before = not (first and k == 0)
                    s_t, t = s + (k // TILE_CHUNKS + 1) // 2, (k // TILE_CHUNKS + 1) % 2
                    uses = dict(shared_uses(k, first, is_last(s)))
                    k1 = (k - 1) % CHUNKS
                    if before:
                        store_cin1(c - 1, k1)
                    for g in range(GROUPS):
                        use = uses.get(g)
                        if use and "turn" in use:
                            store_cols(s_t, t, int(use[-1]), turn_ps)
                        ka, ga = divmod(GROUPS * k + g + HIGH_AHEAD, GROUPS)
                        if not (is_last(s) and ka == CHUNKS):
                            round_pairs(CHUNKS * s + ka, ka, ga)
                        if g == REPEAT_AT:
                            for ahead in rotated(k, first, is_last(s)):
                                repeat_base(s, k + ahead)
                        if g == TURN_X1_AT and before:
                            store_x1(c - 1, k1)
                        quarter = taken(k, g, first, is_last(s))
                        if quarter is not None:
                            repeat_rows(s_t, t, quarter)
                        if g >= MOMENTS_AT and before:
                            store_moments(c - 1, k1, g - MOMENTS_AT)
                        if top_step(s, k, g) is not None:
                            TOP_STEPS[top_step(s, k, g)](s - 1)
                    if k == TILE_CHUNKS - 1 and not first:
                        store_sums(s - 1, 1)
                        store_cin2(s - 1, 1)
                    if k == 2 * TILE_CHUNKS - 1:
                        store_sums(s, 0)
                        store_cin2(s, 0)

            act.wait_ge(dense_loaded, 32)
            nc.scalar.copy(dense_parts[:, 0, :], dense_raw).then_inc(dense_split, 1)
            act.wait_ge(dense_split, 2)
            nc.scalar.copy(dense_parts[:, 1, :], dense_rest).then_inc(dense_split, 1)
            act.wait_ge(w0_ready, 1)
            nc.scalar.copy(w0_high[:, :, :], w0_sb[:, :, :]).then_inc(w0_ready, 1)
            act.wait_ge(w0_ready, 3)
            nc.scalar.copy(w0_low[:LAST_ROWS, LAST:, :], w0_high[:LAST_ROWS, LAST:, :]).then_inc(w0_ready, 1)
            for quarter in range(QUARTERS):
                repeat_rows(0, 0, quarter)
            act.wait_ge(dense_ready, 2 * 16 * len(DENSE_PAIRS))
            for quarter in range(QUARTERS):
                store_cols(0, 0, quarter, first_turn_ps[quarter])
            repeat_base(0, 0)
            repeat_base(0, 1)
            for g in range(HIGH_AHEAD):
                round_pairs(0, 0, g)
            act.wait_ge(top_loaded, 5 * 16)
            over_superblocks(act, superblock)
            c = N_SUPER * CHUNKS - 1
            store_cin1(c, CHUNKS - 1)
            store_x1(c, CHUNKS - 1)
            for j in range(SUBS):
                store_moments(c, CHUNKS - 1, j)
            store_sums(N_SUPER - 1, 1)
            store_cin2(N_SUPER - 1, 1)
            hidden1(N_SUPER - 1, 0, end_hidden1[:2])
            hidden1(N_SUPER - 1, 1, end_hidden1[2:])
            hidden2(N_SUPER - 1, end_hidden2)
            store_result(N_SUPER - 1)

        @block.vector
        def _(dve):
            def multiply(s, k, g):
                c = CHUNKS * s + k
                n, nk = GROUPS * c + g, GROUPS * k + g
                a, b = SLOT_PAIRS[g]
                slot = [base_of(k)] + [slots[:, k % 2, u, :] for u in range(SLOTS - 1)]
                if g == 0:
                    dve.wait_ge(cols_done, cols_of(s, k))
                if a == 0:
                    dve.wait_ge(slot_loaded[k % 2][b], SLOT_DMAS[b] * (CHUNKS // 2 * s + k // 2 + 1))
                at_least(dve, pairs_split, n + 1 - PAIR_BUFS)
                nc.vector.tensor_tensor(pairs[:, nk % PAIR_BUFS, :], slot[a], slot[b],
                                        ALU.mult).then_inc(pairs_done, 1)

            def low_pairs(c, k, g):
                n, bp, r = GROUPS * c + g, (GROUPS * k + g) % PAIR_BUFS, LAST_ROWS if g == LAST else ROWS
                dve.wait_ge(pairs_rounded, n + 1)
                at_least(dve, pairs_used, n + 1 - GROUPS)
                nc.vector.tensor_tensor(pairs_low[:r, g, :], pairs[:r, bp, :], pairs_high[:r, g, :].bitcast(F32),
                                        ALU.subtract).then_inc(pairs_split, 1)

            def fill_diagonal(c, k):
                dve.wait_ge(diag_turned, c + 1)
                at_least(dve, mom_sum, SUBS * (c - 1))
                fields = misc_ps[:, :SUBS * FIELDS].rearrange("p (j m) -> p j m", m=FIELDS)
                shape = [P, SUBS, SUB_SAMPLES, FIELDS]
                nc.vector.tensor_tensor(
                    diag[:, k % 2, :, :, 0:FIELDS], fields.unsqueeze(2).to_broadcast(shape),
                    mask_sb[:, :].unsqueeze(1).unsqueeze(3).to_broadcast(shape), ALU.mult,
                ).then_inc(diag_done, 1)

            def take_indices(s, b):
                nc.vector.tensor_copy(idx_sb[:, b], ids_sb[:, bass.ds(2 * s, 2), :]).then_inc(idx_ready, 1)

            dve.wait_ge(ids_loaded, 16)
            take_indices(0, 0)
            take_indices(1, 1)
            dve.wait_ge(ones_ready, 2)
            dve.wait_ge(const_loaded, 32)
            for b in range(2):
                nc.vector.tensor_copy(diag[:, b, :, :, FIELDS],
                                      mask_sb[:, :].unsqueeze(1).to_broadcast([P, SUBS, SUB_SAMPLES])).then_inc(ones_ready, 1)
            dve.wait_ge(dense_split, 1)
            nc.vector.tensor_tensor(dense_rest, dense_raw, dense_parts[:, 0, :], ALU.subtract).then_inc(dense_split, 1)
            dve.wait_ge(dense_split, 3)
            nc.vector.tensor_tensor(dense_parts[:, 2, :], dense_rest, dense_parts[:, 1, :], ALU.subtract).then_inc(dense_split, 1)
            dve.wait_ge(pair_loaded, 16)
            nc.vector.tensor_tensor(w0_sb[:, :, :], pair_raw[:, :, 0, :], pair_raw[:, :, 1, :], ALU.add).then_inc(w0_ready, 1)
            dve.wait_ge(w0_ready, 2)
            nc.vector.tensor_tensor(w0_low[:, :, :], w0_sb[:, :, :], w0_high[:, :, :].bitcast(F32),
                                    ALU.subtract).then_inc(w0_ready, 1)

            def superblock(s):
                first = isinstance(s, int) and s == 0
                for k in chunk_range(s):
                    c = CHUNKS * s + k
                    for g in range(GROUPS):
                        multiply(s, k, g)
                        if g >= LOW_LAG:
                            low_pairs(c, k, g - LOW_LAG)
                        elif not (first and k == 0):
                            low_pairs(c - 1, (k - 1) % CHUNKS, GROUPS + g - LOW_LAG)
                        if g == (DIAG_EARLY if k % TILE_CHUNKS == 2 else DIAG_AT):
                            fill_diagonal(c, k)
                    if k == 3 and not is_last(s):
                        for tile in range(2):
                            dve.wait_ge(gathered[tile], GATHERED * (s + 1))
                        take_indices(s + 2, s % 2)

            over_superblocks(dve, superblock)
            for g in range(GROUPS - LOW_LAG, GROUPS):
                low_pairs(N_SUPER * CHUNKS - 1, CHUNKS - 1, g)

        @block.tensor
        def _(pe):
            mm = nc.tensor.matmul

            def turn(tile, quarter, turned_ps):
                pe.wait_ge(rows_done, QUARTERS * tile + quarter + 1)
                for i in range(TURN):
                    last = nc.tensor.transpose(turned_ps[:ROWS, i, :],
                                               rows[:, quarter * TURN + i].rearrange("p a m -> p (a m)"), ident_sb[:, :])
                last.then_inc(turned, 1)

            def turn_diagonal(k):
                for j in range(SUBS):
                    last = nc.tensor.transpose(misc_ps[:, j * FIELDS:(j + 1) * FIELDS],
                                               base_of(k)[:FIELDS, j * P:(j + 1) * P], ident_sb[:FIELDS, :FIELDS])
                last.then_inc(diag_turned, 1)

            def cin1(c, k, g):
                pe.wait_ge(pairs_split, GROUPS * c + g + 1)
                if g == 0:
                    at_least(pe, cin1_done, c - 1)
                if g == LAST:
                    mm(cin1_ps[k % 2][:, :], w0_low[:, LAST, :], pairs_high[:, g, :], start=False, stop=False)
                    pe.wait_ge(high_copied, 16 * (c + 1))
                    last = mm(cin1_ps[k % 2][:, :], w0_low[:, LAST + 1, :], pairs_low[:, g, :], start=False, stop=True)
                else:
                    mm(cin1_ps[k % 2][:, :], w0_high[:, g, :], pairs_high[:, g, :], start=(g == 0), stop=False)
                    mm(cin1_ps[k % 2][:, :], w0_low[:, g, :], pairs_high[:, g, :], start=False, stop=False)
                    last = mm(cin1_ps[k % 2][:, :], w0_high[:, g, :], pairs_low[:, g, :], start=False, stop=False)
                last.then_inc(pairs_used, 1)

            def turn_x1(c):
                pe.wait_ge(cin1_done, c + 1)
                at_least(pe, x1_done, c)
                for j in range(SUBS):
                    last = nc.tensor.transpose(x1_ps[:, j * OUT:(j + 1) * OUT], x1_turned[:, j * P:(j + 1) * P],
                                               ident_sb[:, :])
                last.then_inc(x1_turn, 1)

            def sum_moments(c, k, j):
                if j == 0:
                    pe.wait_ge(x1_done, c + 1)
                    pe.wait_ge(diag_done, c + 1)
                at_least(pe, mom_done, SUBS * c + j - 1)
                mm(mom_ps[j % 2][:, :MOM], x1_sb[:, k % 2, j * OUT:(j + 1) * OUT], diag[:, k % 2, j, :, :],
                   start=True, stop=True).then_inc(mom_sum, 1)

            def cin2(s, t, fields):
                for m in fields:
                    if m == 0:
                        pe.wait_ge(mom_done, SUBS * TILE_CHUNKS * (2 * s + t + 1))
                        at_least(pe, res_done, 2 * (2 * s + t))
                    last = mm(cin2_ps[:, :], w1_sb[:, m, :], moments[:, t, m, :], start=(m == 0), stop=(m == FIELDS - 1))
                    if m == FIELDS - 1:
                        last.then_inc(cin2_sum, 1)

            def hidden1(s, half):
                if half:
                    pe.wait_ge(hid1_done, 4 * s + 2)
                else:
                    pe.wait_ge(res_done, 4 * (s + 1))
                    at_least(pe, y_done, s)
                for j in range(2):
                    o = (2 * half + j) * P
                    for i in range(2):
                        mm(top_ps[:, j, :], top1a_sb[:, i, o:o + P], res_sb[:, i, :], start=(i == 0), stop=False)
                    last = mm(top_ps[:, j, :], dense_sb[:, BATCH + o:BATCH + o + P],
                              dense_sb[:, bass.ds(s * SUPER, SUPER)], start=False, stop=True)
                last.then_inc(hid1_sum, 1)

            def hidden2(s):
                pe.wait_ge(hid1_done, 4 * (s + 1))
                for j in range(HID2 // P):
                    for i in range(HID1 // P):
                        last = mm(top_ps[:, j, :], top2_sb[:, i, j * P:(j + 1) * P], hid1_sb[:, i, :],
                                  start=(i == 0), stop=(i == HID1 // P - 1))
                last.then_inc(hid2_sum, 1)

            def result(s):
                pe.wait_ge(hid2_done, 2 * (s + 1))
                for i in range(HID2 // P):
                    last = mm(top_ps[0:1, 0, :], top3_sb[:, i:i + 1], hid2_sb[:, i, :],
                              start=(i == 0), stop=(i == HID2 // P - 1))
                last.then_inc(y_sum, 1)

            TOP_STEPS = [lambda s: hidden1(s, 0), lambda s: hidden1(s, 1), hidden2, result]

            pe.wait_ge(const_loaded, 32)
            for quarter in range(QUARTERS):
                turn(0, quarter, first_turn_ps[quarter])
            pe.wait_ge(w0_ready, 4)
            pe.wait_ge(ones_ready, 4)
            pe.wait_ge(w1_loaded, 16)
            pe.wait_ge(top_loaded, 5 * 16)
            pe.wait_ge(dense_ready, 2 * 16 * len(DENSE_PAIRS))

            def shared_use(s, k, use):
                first, last = isinstance(s, int) and s == 0, is_last(s)
                uses = [u for _, u in shared_uses(k, first, last)]
                c = CHUNKS * s + k
                if use != uses[0]:
                    prior, kp = uses[uses.index(use) - 1], k
                elif first and k == 0:
                    prior, kp = "turn3", -1
                else:
                    prior, kp = shared_uses((k - 1) % CHUNKS, first, last and k > 0)[-1][1], k - 1
                if prior == "diag":
                    pe.wait_ge(diag_done, c - k + kp + 1)
                else:
                    pe.wait_ge(cols_done, QUARTERS * (2 * s + kp // TILE_CHUNKS + 1) + int(prior[-1]) + 1)
                if use != "diag":
                    turn(2 * s + k // TILE_CHUNKS + 1, int(use[-1]), turn_ps)

            def superblock(s):
                first = isinstance(s, int) and s == 0
                for k in chunk_range(s):
                    c = CHUNKS * s + k
                    before = not (first and k == 0)
                    uses = dict(shared_uses(k, first, is_last(s)))
                    for g in range(GROUPS):
                        if g in uses:
                            shared_use(s, k, uses[g])
                        cin1(c, k, g)
                        if uses.get(g) == "diag":
                            turn_diagonal(k)
                        if g == TURN_X1_AT and before:
                            turn_x1(c - 1)
                        if g >= MOMENTS_AT and before:
                            sum_moments(c - 1, (k - 1) % CHUNKS, g - MOMENTS_AT)
                        slot = (k % TILE_CHUNKS - 1) * GROUPS + g - CIN2_AT
                        if slot >= 0 and not (first and k < TILE_CHUNKS):
                            fields = range(slot * CIN2_STEP, min(FIELDS, (slot + 1) * CIN2_STEP))
                            if k < TILE_CHUNKS:
                                cin2(s - 1, 1, fields)
                            else:
                                cin2(s, 0, fields)
                        if top_step(s, k, g) is not None:
                            TOP_STEPS[top_step(s, k, g)](s - 1)

            over_superblocks(pe, superblock)
            c = N_SUPER * CHUNKS - 1
            turn_x1(c)
            for j in range(SUBS):
                sum_moments(c, CHUNKS - 1, j)
            end = N_SUPER - 1
            pe.wait_ge(y_done, end)
            for o in range(HID1 // P):
                mm(end_hidden1[o], dense_sb[:, BATCH + o * P:BATCH + (o + 1) * P],
                   dense_sb[:, end * SUPER:BATCH], start=True, stop=False)
            cin2(end, 1, range(FIELDS))
            for i in range(2):
                pe.wait_ge(res_done, 4 * end + 3 + i)
                for o in range(HID1 // P):
                    last = mm(end_hidden1[o], top1a_sb[:, i, o * P:(o + 1) * P], res_sb[:, i, :],
                              start=False, stop=(i == 1))
                    if i == 1 and o % 2:
                        last.then_inc(hid1_sum, 1)
            for i in range(HID1 // P):
                pe.wait_ge(hid1_done, 4 * end + i + 1)
                for j in range(HID2 // P):
                    last = mm(end_hidden2[j], top2_sb[:, i, j * P:(j + 1) * P], hid1_sb[:, i, :],
                              start=(i == 0), stop=(i == HID1 // P - 1))
            last.then_inc(hid2_sum, 1)
            result(end)


def pair_rows():
    j, m = np.divmod(np.arange(ROWS), FIELDS)
    turn = np.array(ROTATIONS)[j]
    a, b = np.array(SLOT_PAIRS).T
    first, second = turn[:, a], turn[:, b]
    repeated = np.where(j == PARTS - 1, ROTATIONS[1][SLOTS - 1], second[:, LAST])
    x = (m[:, None] + np.c_[first, first[:, LAST]]) % FIELDS
    y = (m[:, None] + np.c_[second, repeated]) % FIELDS
    return x * FIELDS + y, y * FIELDS + x, x == y


def kernel(**inputs):
    import concourse.bacc as bacc
    from concourse.bass_utils import run_bass_kernel_spmd

    a = {k: np.ascontiguousarray(v) for k, v in inputs.items()}
    w0, rows = a["L0_rec_W0"], pair_rows()
    pair_w = np.stack([w0[rows[0]], w0[rows[1]]], axis=2)
    pair_w[rows[2], 1] = 0
    arrays = {
        "dense_t": a["dense_ctx"].T,
        "ids": np.pad(a["ids"], ((0, SUPER), (0, 0))).reshape(-1, TILE, FIELDS).transpose(1, 0, 2),
        **{f"tbl_{f}": a[f"tbl_{f}"] for f in range(FIELDS)},
        "pair_w": pair_w,
        "w1": a["L0_rec_W1"].reshape(FIELDS, OUT, OUT).transpose(1, 0, 2),
        "w_top1a": a["W_top1"][:2 * P].reshape(2, P, HID1).transpose(1, 0, 2),
        "w_top1b": a["W_top1"][2 * P:],
        "b_top1": a["b_top1"].reshape(HID1 // P, P).T,
        "w_top2": a["W_top2"].reshape(HID1 // P, P, HID2).transpose(1, 0, 2),
        "b_top2": a["b_top2"].reshape(HID2 // P, P).T,
        "w_top3": a["W_top3"][:, 0].reshape(HID2 // P, P).T,
        "ident_const": np.eye(P, dtype=np.float32),
        "mask_const": (np.arange(P)[:, None] // DIM == np.arange(SUB_SAMPLES)).astype(np.float32),
    }
    arrays = {f"in_{k}": np.ascontiguousarray(v) for k, v in arrays.items()}
    nc = bacc.Bacc("TRN2", target_bir_lowering=False, num_devices=1)
    ap = {k[3:]: nc.dram_tensor(k, v.shape, mybir.dt.from_np(v.dtype), kind="ExternalInput").ap()
          for k, v in arrays.items()}
    out = nc.dram_tensor("out_y", (BATCH, 1), F32, kind="ExternalOutput").ap()
    tower(nc, ap["dense_t"], ap["ids"], [ap[f"tbl_{f}"] for f in range(FIELDS)], ap["pair_w"], ap["w1"],
          ap["w_top1a"], ap["w_top1b"], ap["b_top1"], ap["w_top2"], ap["b_top2"], ap["w_top3"],
          ap["ident_const"], ap["mask_const"], out)
    r = run_bass_kernel_spmd(nc, [arrays], core_ids=[0])
    return r.results[0]["out_y"]
```
